# Optimizing a Trainium2 kernel written in Bass

```python
import numpy as np
import jax
import jax.numpy as jnp

def _softmax(x, axis=-1):
    return jax.nn.softmax(x, axis=axis)

def _gelu(x):
    return jax.nn.gelu(x, approximate=True)

def _silu(x):
    return jax.nn.silu(x)

def _sigmoid(x):
    return jax.nn.sigmoid(x)

def _layernorm(x, axis=-1, eps=1e-05):
    m = jnp.mean(x, axis=axis, keepdims=True)
    v = jnp.var(x, axis=axis, keepdims=True)
    return (x - m) / jnp.sqrt(v + eps)

def _scatter_add(tgt, idx, src, axis=0):
    return tgt.at[idx].add(src)

def _segment_sum(src, seg, n):
    return jax.ops.segment_sum(src, seg, n)
kernel_name = 'mk_gnn_preln_d2_gnn_r8_5fbe4b'

def setup_inputs(seed: int=0):
    np.random.seed(seed)
    _w = jnp.asarray

    def _rec_inputs():
        import jax
        import jax.numpy as jnp
        _gk = jax.random.key(seed)
        x = -8.776e-05 + 1 * jax.random.normal(jax.random.fold_in(_gk, 1), (1250, 512), jnp.float32)
        src = jax.random.randint(jax.random.fold_in(_gk, 2), (40000,), 0, 1250, jnp.int32)
        dst = jnp.minimum((1250 * jax.random.uniform(jax.random.fold_in(_gk, 3), (40000,)) ** 2.0).astype(jnp.int32), 9999)
        _o = jnp.argsort(dst, stable=True)
        src = src[_o]
        dst = dst[_o]
        edge_attr_512 = -8.513e-05 + 0.999844 * jax.random.normal(jax.random.fold_in(_gk, 12), (40000, 512), jnp.float32)
        return (x, src, dst, edge_attr_512)
    x, src, dst, edge_attr_512 = _rec_inputs()

    def _L0_gnn_setup():
        import jax, jax.numpy as jnp
        import numpy as np
        N = 1250
        E = 20000
        D = 512
        key = jax.random.key(seed)
        k1, k2, k3, k4, k5 = jax.random.split(key, 5)
        node_tokens = jax.random.normal(k1, (N, D), dtype=jnp.float32)
        relation_tokens = jax.random.normal(k2, (E, D), dtype=jnp.float32)
        edge_index = jax.random.randint(k3, (2, E), 0, N, dtype=jnp.int64)
        lim_m = float(np.sqrt(6.0 / (D + D)))
        Wm = jax.random.uniform(k4, (D, D), minval=-lim_m, maxval=lim_m, dtype=jnp.float32)
        bm = jnp.zeros((D,), dtype=jnp.float32)
        lim_u = float(np.sqrt(6.0 / (2 * D + D)))
        Wu = jax.random.uniform(k5, (D, 2 * D), minval=-lim_u, maxval=lim_u, dtype=jnp.float32)
        bu = jnp.zeros((D,), dtype=jnp.float32)
        gamma = jnp.ones((D,), dtype=jnp.float32)
        beta = jnp.zeros((D,), dtype=jnp.float32)
        return {'node_tokens': node_tokens, 'relation_tokens': relation_tokens, 'edge_index': edge_index, 'num_nodes': N, 'Wm': Wm, 'bm': bm, 'Wu': Wu, 'bu': bu, 'gamma': gamma, 'beta': beta}
    _L0_gnn_all = _L0_gnn_setup()
    _L0_gnn_in = {k: v for k, v in _L0_gnn_all.items() if k in ('Wm', 'bm', 'Wu', 'bu', 'gamma', 'beta')}
    del _L0_gnn_all

    def _L1_gnn_setup():
        import jax, jax.numpy as jnp
        import numpy as np
        N_NODES = 1250
        N_EDGES = 20000
        D_IN = 512
        D_HID = 1024
        key = jax.random.key(seed)
        ks = jax.random.split(key, 8)
        feat = jax.random.normal(ks[0], (N_NODES, D_IN), dtype=jnp.float32)
        W1 = jax.random.normal(ks[1], (D_IN, D_HID), dtype=jnp.float32) * (1.0 / np.sqrt(D_IN))
        b1 = jnp.zeros((D_HID,), dtype=jnp.float32)
        W2 = jax.random.normal(ks[2], (D_HID, D_IN), dtype=jnp.float32) * (1.0 / np.sqrt(D_HID))
        b2 = jnp.zeros((D_IN,), dtype=jnp.float32)
        eps = jnp.zeros((1,), dtype=jnp.float32)
        src = jax.random.randint(ks[3], (N_EDGES,), 0, N_NODES, dtype=jnp.int32)
        dst = jax.random.randint(ks[4], (N_EDGES,), 0, N_NODES, dtype=jnp.int32)
        return {'feat': feat, 'W1': W1, 'b1': b1, 'W2': W2, 'b2': b2, 'eps': eps, 'src': src, 'dst': dst}
    _L1_gnn_all = _L1_gnn_setup()
    _L1_gnn_in = {k: v for k, v in _L1_gnn_all.items() if k in ('W1', 'b1', 'W2', 'b2', 'eps')}
    del _L1_gnn_all
    return {'x': x, 'src': src, 'dst': dst, 'edge_attr_512': edge_attr_512, 'L0_gnn_Wm': _L0_gnn_in['Wm'], 'L0_gnn_bm': _L0_gnn_in['bm'], 'L0_gnn_Wu': _L0_gnn_in['Wu'], 'L0_gnn_bu': _L0_gnn_in['bu'], 'L0_gnn_gamma': _L0_gnn_in['gamma'], 'L0_gnn_beta': _L0_gnn_in['beta'], 'L1_gnn_W1': _L1_gnn_in['W1'], 'L1_gnn_b1': _L1_gnn_in['b1'], 'L1_gnn_W2': _L1_gnn_in['W2'], 'L1_gnn_b2': _L1_gnn_in['b2'], 'L1_gnn_eps': _L1_gnn_in['eps']}

def reference(x, src, dst, edge_attr_512, L0_gnn_Wm, L0_gnn_bm, L0_gnn_Wu, L0_gnn_bu, L0_gnn_gamma, L0_gnn_beta, L1_gnn_W1, L1_gnn_b1, L1_gnn_W2, L1_gnn_b2, L1_gnn_eps):
    import jax
    import jax.numpy as jnp

    def _L0_gnn_ref(node_tokens, relation_tokens, edge_index, num_nodes, Wm, bm, Wu, bu, gamma, beta):
        import jax, jax.numpy as jnp
        import numpy as np
        N = 1250
        E = 20000
        D = 512
        head = edge_index[0]
        tail = edge_index[1]
        msg = node_tokens[head] + relation_tokens
        msg = msg @ Wm.T + bm
        agg = jax.ops.segment_sum(msg, tail, num_segments=num_nodes)
        deg = jax.ops.segment_sum(jnp.ones((msg.shape[0],), dtype=msg.dtype), tail, num_segments=num_nodes)
        agg = agg / jnp.maximum(deg, 1.0)[:, None]
        update_in = jnp.concatenate((node_tokens, agg), axis=-1)
        update = update_in @ Wu.T + bu
        out = node_tokens + jax.nn.gelu(update, approximate=False)
        mean = jnp.mean(out, axis=-1, keepdims=True)
        var = jnp.var(out, axis=-1, keepdims=True)
        return (out - mean) / jnp.sqrt(var + 1e-05) * gamma + beta

    def _L1_gnn_ref(feat, W1, b1, W2, b2, eps, src, dst):
        import jax, jax.numpy as jnp
        import numpy as np
        N_NODES = 1250
        N_EDGES = 20000
        D_IN = 512
        D_HID = 1024
        msgs = feat[src]
        neigh = jax.ops.segment_sum(msgs, dst, num_segments=feat.shape[0])
        rst = (1.0 + eps[0]) * feat + neigh
        h = jnp.maximum(rst @ W1 + b1, 0.0)
        h = h @ W2 + b2
        return h + feat
    edge_index = jnp.stack([src, dst])
    h = jnp.maximum(_layernorm(x, axis=-1), 0.0)
    x = x + _L0_gnn_ref(h, edge_attr_512, edge_index, 1250, L0_gnn_Wm, L0_gnn_bm, L0_gnn_Wu, L0_gnn_bu, L0_gnn_gamma, L0_gnn_beta)
    h = jnp.maximum(_layernorm(x, axis=-1), 0.0)
    x = x + _L1_gnn_ref(h, L1_gnn_W1, L1_gnn_b1, L1_gnn_W2, L1_gnn_b2, L1_gnn_eps, src, dst)
    return x

_drawn_inputs = setup_inputs


def setup_inputs(seed=0):
    import zlib

    import numpy as np

    out = dict(_drawn_inputs(seed))
    spreads = {'L0_gnn_bm': (0.0, 0.1),
     'L0_gnn_bu': (0.0, 0.1),
     'L0_gnn_gamma': (1.0, 0.2),
     'L0_gnn_beta': (0.0, 0.1),
     'L1_gnn_b1': (0.0, 0.8),
     'L1_gnn_b2': (0.0, 0.8)}
    factors = {'edge_attr_512': 2.818}
    for name, (base, spread) in spreads.items():
        noise = np.random.default_rng([zlib.crc32(name.encode()), seed]).standard_normal(out[name].shape)
        drawn = base * np.exp(spread * noise) if base else spread * noise
        out[name] = jnp.asarray(drawn.astype(out[name].dtype))
    for name, factor in factors.items():
        out[name] = (out[name] * factor).astype(out[name].dtype)
    return out
```

```python
from contextlib import ExitStack

import concourse.bass as bass
from concourse import mybir

F32 = mybir.dt.float32
F32R = mybir.dt.float32r
BF16 = mybir.dt.bfloat16
I32 = mybir.dt.int32
U16 = mybir.dt.uint16
ALU = mybir.AluOpType
ACT = mybir.ActivationFunctionType
AX = mybir.AxisListType

P = 128
SUB = 4
SLOTS = 3
W = 12
HALF = 64
EPS = 1e-5
PREP_OFFS = 18
PREP_KEYS = 29
PREP_ALL = 32


def gnn_kernel(nc, x, src, dst, edge, Wm, bm, Wu, bu, gamma, beta, W1, b1, W2, b2, eps, out):
    N, D = x.shape
    E = edge.shape[0]
    HID = W1.shape[1]
    NT = -(-N // P)
    NP = NT * P
    TAIL = N - (NT - 1) * P
    FC = D // P
    KC = HID // P
    GE = SUB * P
    NG = -(-E // GE)
    ETAIL = E - (NG - 1) * GE
    GP = NG + 1
    HB = NT
    KW = HB * W
    NW = (NP - P) // HALF + 1
    AW = NP + W
    QC = 256
    NQ = NP // QC
    NCONV = NT
    assert (NG - 1) % SLOTS == 0 and ETAIL % SUB == 0 and D == GE and NQ == 5

    at = [-(-nc.sbuf_base // 64) * 64]

    def place(name, shape, dt, offset=None):
        size = mybir.dt.size(dt)
        for n in shape[1:]:
            size *= n
        if offset is None:
            offset = at[0]
            at[0] += -(-size // 32) * 32
        return nc.alloc_sbuf_tensor_at(name, shape, dt, offset=offset), offset

    H, _ = place("H", [P, NT, D], F32)
    U, _ = place("U", [P, NT, D], F32)
    A16, a16_at = place("A16", [P, HB, AW], U16)
    SW, sw_at = place("SW", [P, NW, D], F32)
    CT, _ = place("CT", [P, FC, D], F32)
    SLOT_BYTES = SUB * D * 4 + 2 * 2 * D * 4 + SUB * P * 4 + SUB * P * 2 + SUB * KW * 2
    stream_at = at[0]
    at[0] += SLOTS * SLOT_BYTES
    ea, hi, lo, oneD, oneS, oneK = [], [], [], [], [], []
    for s in range(SLOTS):
        o = stream_at + s * SLOT_BYTES
        for lst, name, shape, dt in ((ea, "ea", [P, SUB, D], F32), (hi, "hi", [P, 2, D], F32R),
                                     (lo, "lo", [P, 2, D], F32R), (oneD, "oneD", [P, SUB, P], F32R),
                                     (oneS, "oneS", [P, SUB, P], BF16), (oneK, "oneK", [P, SUB, KW], BF16)):
            t, _ = place(f"{name}{s}", shape, dt, o)
            lst.append(t)
            size = mybir.dt.size(dt)
            for n in shape[1:]:
                size *= n
            o += size
    WuN, _ = place("WuN", [P, FC, 2 * D], F32, stream_at)
    WmN, _ = place("WmN", [P, FC, D], F32, stream_at + 16384)
    WuT, _ = place("WuT", [P, 2 * FC, D], F32, stream_at + 24576)
    AF, _ = place("AF", [P, NT, NP], F32, stream_at)
    hid, _ = place("hid", [P, KC, NP], F32, stream_at)
    spare = stream_at + NT * NP * 4
    gammaB, _ = place("gammaB", [P, D], F32, spare)
    betaB, _ = place("betaB", [P, D], F32, spare + 2048)
    b2B, _ = place("b2B", [P, D], F32, spare + 4096)
    assert spare + 6144 <= stream_at + SLOTS * SLOT_BYTES
    aggT, _ = place("aggT", [P, FC, NP], F32, a16_at)
    W1s, _ = place("W1s", [P, FC, HID], F32, sw_at)
    W2s, _ = place("W2s", [P, KC, D], F32, sw_at + 16384)
    g_tmp = {}
    for n, name in enumerate(["dst_f", "bigE", "bigA", "valid", "drel", "wrel", "dE", "dA", "hi_f", "lo_f", "key", "tmp"]):
        g_tmp[name], _ = place("g_" + name, [P, GE], F32, a16_at + n * 2048)
    dst_f, bigE, bigA, valid, drel, wrel, dE, dA, hi_f, lo_f, key, tmpf = g_tmp.values()
    dst_i, _ = place("dst_i", [P, GE], I32, sw_at)
    src_i, _ = place("src_i", [P, GE], I32, sw_at + 2048)
    hi_i, _ = place("hi_i", [P, GE], I32, sw_at + 4096)
    lo_i, _ = place("lo_i", [P, GE], I32, sw_at + 6144)
    idxT = {n: place("T_" + n, [P, SUB, GP], F32)[0] for n in ("drel", "key", "lo", "dE", "dA", "hi")}
    iotaF, _ = place("iotaF", [P, P], F32)
    iotaB, _ = place("iotaB", [P, P], BF16)
    ident, _ = place("ident", [P, P], F32)
    pid, _ = place("pid", [P, 1], F32)
    onesF, _ = place("onesF", [P, 1], F32)
    mhalf, _ = place("mhalf", [P, NT], F32)
    buB, _ = place("buB", [P, D], F32)
    cbB, _ = place("cbB", [P, D], F32)
    bmC, _ = place("bmC", [P, FC], F32)
    bmB, _ = place("bmB", [P, FC, P], F32)
    b1C, _ = place("b1C", [P, KC], F32)
    epsC, _ = place("epsC", [P, 1], F32)
    eps1, _ = place("eps1", [P, 1], F32)
    m4, _ = place("m4", [P, 8], F32)
    wf, _ = place("wf", [P, 4], F32)
    wi, _ = place("wi", [P, 2], I32)
    offs, _ = place("offs", [P, 8], I32)
    offrow, _ = place("offrow", [1, NG * 8], I32)
    nunc_f, _ = place("nunc_f", [1, 2], F32)
    nunc, _ = place("nunc", [1, 2], I32)
    stats, _ = place("stats", [P, NT, 6], F32)
    mv, _ = place("mv", [P, NT, 2], F32)
    mv2, _ = place("mv2", [P, NT, 2], F32)
    ve, _ = place("ve", [P, NT], F32)
    ve2, _ = place("ve2", [P, NT], F32)
    rs, _ = place("rs", [P, NT], F32)
    rs2, _ = place("rs2", [P, NT], F32)
    nb, _ = place("nb", [P, NT], F32)
    degs, _ = place("degs", [P, NT], F32)
    rdeg, _ = place("rdeg", [P, NT], F32)
    has, _ = place("has", [P, NT], F32)
    TB = 3
    tt = [place(f"tt{i}", [P, D], F32)[0] for i in range(TB)]
    xt = [place(f"xt{i}", [P, D], F32)[0] for i in range(TB)]
    Dsum, _ = place("Dsum", [P, NP], F32)
    assert at[0] <= nc.sbuf_usable_end, at[0] - nc.sbuf_usable_end

    ctx = ExitStack()
    with ctx:
        ps = ctx.enter_context(nc.psum_tensor("ps", [P, 8, 512], F32))

        def sem(name):
            return ctx.enter_context(nc.semaphore(name))

        pads_set = sem("pads_set")
        consts = sem("consts")
        idx_in = sem("idx_in")
        x_in = sem("x_in")
        wu_in = sem("wu_in")
        wm_in = sem("wm_in")
        small_in = sem("small_in")
        prep = sem("prep")
        ident_ready = sem("ident_ready")
        offs_in = sem("offs_in")
        a_zero = sem("a_zero")
        idxT_mm = sem("idxT_mm")
        idxT_done = sem("idxT_done")
        wuT_mm = sem("wuT_mm")
        wuT_done = sem("wuT_done")
        ln0 = sem("ln0")
        ve_ready = sem("ve_ready")
        rs_ready = sem("rs_ready")
        nb_ready = sem("nb_ready")
        h0_ready = sem("h0_ready")
        hT_mm = sem("hT_mm")
        hT_done = sem("hT_done")
        u1_mm = sem("u1_mm")
        u1_done = sem("u1_done")
        bmB_done = sem("bmB_done")
        ct_mm = sem("ct_mm")
        ct_done = sem("ct_done")
        group_done = sem("group_done")
        ea_in = [sem(f"ea_in{s}") for s in range(SLOTS)]
        hi_ready = sem("hi_ready")
        lo_ready = sem("lo_ready")
        hot_ready = sem("hot_ready")
        psum_free = sem("psum_free")
        add_step = sem("add_step")
        gen_ea_in = sem("gen_ea_in")
        gen_hot = sem("gen_hot")
        gen_mm = sem("gen_mm")
        gen_add = sem("gen_add")
        gen_step = sem("gen_step")
        summed = sem("summed")
        conv = [sem("conv_act"), sem("conv_dve")]
        dsum_ready = sem("dsum_ready")
        deg_mm = sem("deg_mm")
        deg_step = sem("deg_step")
        win_mm = sem("win_mm")
        win_add = sem("win_add")
        agg_mm = sem("agg_mm")
        agg_done = sem("agg_done")
        c_mm = sem("c_mm")
        t_ready = sem("t_ready")
        g_ready = sem("g_ready")
        o_step = sem("o_step")
        ve1_ready = sem("ve1_ready")
        rs1_ready = sem("rs1_ready")
        ve2_ready = sem("ve2_ready")
        rs2_ready = sem("rs2_ready")
        x1_ready = sem("x1_ready")
        nb2_ready = sem("nb2_ready")
        h1_ready = sem("h1_ready")
        late_in = sem("late_in")
        w12_in = sem("w12_in")
        xt_in = [sem(f"xt_in{i}") for i in range(TB)]
        xb_ready = sem("xb_ready")
        h1T_mm = sem("h1T_mm")
        h1T_done = sem("h1T_done")
        rst_mm = sem("rst_mm")
        rst_done = sem("rst_done")
        hid_mm = sem("hid_mm")
        hid_done = sem("hid_done")
        res_step = sem("res_step")
        y_mm = sem("y_mm")
        y_done = sem("y_done")
        stored = sem("stored")

        block = ctx.enter_context(nc.Block())

        edge_g = edge[0:(NG - 1) * GE, :].rearrange("(g p j) d -> g p j d", p=P, j=SUB)
        edge_tail = edge[(NG - 1) * GE:E, :].rearrange("(p j) d -> p j d", j=SUB)
        TP = ETAIL // SUB

        @block.sync
        def _(sp):
            sp.wait_ge(pads_set, 3)
            for t, a in ((dst_i, dst), (src_i, src)):
                sp.dma_start(t[0:NG - 1, :], a[0:(NG - 1) * GE].rearrange("(g e) -> g e", e=GE)).then_inc(idx_in, 16)
                sp.dma_start(t[NG - 1:NG, 0:ETAIL], a[(NG - 1) * GE:E].rearrange("(g e) -> g e", g=1)).then_inc(idx_in, 16)
            sp.dma_start(H[:, 0:NT - 1, :], x[0:(NT - 1) * P, :].rearrange("(b p) d -> p b d", p=P)).then_inc(x_in, 16)
            sp.dma_start(H[0:TAIL, NT - 1, :], x[(NT - 1) * P:N, :]).then_inc(x_in, 16)
            sp.dma_start(WuN[:], Wu.rearrange("(o p) i -> p o i", p=P)).then_inc(wu_in, 16)
            sp.dma_start(WmN[:], Wm.rearrange("(m p) i -> p m i", p=P)).then_inc(wm_in, 16)
            sp.dma_start(buB[:], bu.rearrange("(a d) -> a d", a=1).broadcast_to([P, D])).then_inc(small_in, 16)
            sp.dma_start(bmC[:], bm.rearrange("(m p) -> p m", p=P), allow_slow_non_contiguous=True).then_inc(small_in, 16)
            sp.dma_start(b1C[:], b1.rearrange("(k p) -> p k", p=P), allow_slow_non_contiguous=True).then_inc(small_in, 16)
            sp.dma_start(epsC[:], eps.rearrange("(a d) -> a d", a=1).broadcast_to([P, 1])).then_inc(small_in, 16)
            sp.wait_ge(prep, PREP_OFFS)
            sp.dma_start(offrow[0:1, :], offs[0:NG, :]).then_inc(offs_in, 16)
            with sp.Fori(0, (NG - 1) // SLOTS) as i:
                for s in range(SLOTS):
                    sp.wait_ge(group_done, i * SLOTS + s + 1)
                    sp.dma_start(ea[s][:], edge_g[bass.ds(i * SLOTS + s, 1)].rearrange("g p j d -> (g p) j d")).then_inc(ea_in[s], 16)
            sp.wait_ge(group_done, NG)
            sp.dma_start(ea[0][0:TP, :, :], edge_tail).then_inc(ea_in[0], 16)

            sp.wait_ge(psum_free, NG + SLOTS)
            sp.wait_ge(prep, PREP_ALL)
            uncovered = sp.value_load(nunc[0:1, 0:1], min_val=0, max_val=2 * E)
            with sp.If(uncovered > 0):
                with sp.Fori(0, NT) as b:
                    with sp.Fori(0, NG - 1) as g:
                        sp.wait_ge(gen_mm, b * NG + g + 1)
                        sp.dma_start(ea[0][:], edge_g[bass.ds(g, 1)].rearrange("g p j d -> (g p) j d")).then_inc(gen_ea_in, 16)
                    sp.wait_ge(gen_mm, b * NG + NG)
                    sp.dma_start(ea[0][0:TP, :, :], edge_tail).then_inc(gen_ea_in, 16)
                sp.nop()

            sp.wait_ge(summed, 1)
            for t, a in ((gammaB, gamma), (betaB, beta), (b2B, b2)):
                sp.dma_start(t[:], a.rearrange("(a d) -> a d", a=1).broadcast_to([P, D])).then_inc(late_in, 16)

            def load_x(b):
                if b >= TB:
                    sp.wait_ge(x1_ready, b - TB + 1)
                if b < NT - 1:
                    sp.dma_start(xt[b % TB][:], x[b * P:(b + 1) * P, :]).then_inc(xt_in[b % TB], 16)
                else:
                    sp.dma_start(xt[b % TB][0:TAIL, :], x[b * P:N, :]).then_inc(xt_in[b % TB], 16)

            for b in range(TB):
                load_x(b)
            sp.wait_ge(win_mm, NW)
            sp.dma_start(W1s[:], W1.rearrange("(f p) h -> p f h", p=P)).then_inc(w12_in, 16)
            sp.dma_start(W2s[:], W2.rearrange("(k p) d -> p k d", p=P)).then_inc(w12_in, 16)
            for b in range(TB, NT):
                load_x(b)
            for b in range(NT):
                rows = P if b < NT - 1 else TAIL
                sp.wait_ge(y_done, b + 1)
                sp.dma_start(out[b * P:b * P + rows, :], U[0:rows, b, :]).then_inc(stored, 16)
            sp.wait_ge(stored, 16 * NT)

        @block.gpsimd
        def _(pool):
            nc.gpsimd.memset(dst_i[:], NP - 1).then_inc(pads_set, 1)
            nc.gpsimd.memset(src_i[:], 0).then_inc(pads_set, 1)
            nc.gpsimd.memset(H[:, NT - 1, :], 0.0).then_inc(pads_set, 1)
            nc.gpsimd.iota(iotaF[:], [[1, P]], base=0, channel_multiplier=0, allow_small_or_imprecise_dtypes=True).then_inc(consts, 1)
            nc.gpsimd.iota(pid[:], [[1, 1]], base=0, channel_multiplier=1, allow_small_or_imprecise_dtypes=True).then_inc(consts, 1)
            nc.gpsimd.iota(iotaB[:], [[1, P]], base=0, channel_multiplier=0, allow_small_or_imprecise_dtypes=True).then_inc(consts, 1)
            nc.gpsimd.memset(mhalf[:], -0.5).then_inc(consts, 1)
            nc.gpsimd.memset(onesF[:], 1.0).then_inc(consts, 1)
            nc.gpsimd.memset(offs[:], 0).then_inc(consts, 1)
            for t in xt:
                nc.gpsimd.memset(t[:], 0.0).then_inc(consts, 1)
            pool.wait_ge(consts, 6 + TB)
            pool.wait_ge(ve_ready, 1)
            nc.gpsimd.tensor_tensor(rs[:], ve[:], mhalf[:], ALU.pow).then_inc(rs_ready, 1)
            pool.wait_ge(prep, PREP_ALL)
            nc.gpsimd.memset(SW[:], 0.0).then_inc(a_zero, 1)

            def low_parts(s, n, turn):
                pool.wait_ge(ea_in[s], 16 * (turn + 1))
                pool.wait_ge(hi_ready, n + 1)
                nc.gpsimd.tensor_tensor(lo[s][:], ea[s][:, 2:4, :], hi[s][:].bitcast(F32), ALU.subtract).then_inc(lo_ready, 1)

            with pool.Fori(0, (NG - 1) // SLOTS) as i:
                for s in range(SLOTS):
                    low_parts(s, i * SLOTS + s, i)
            low_parts(0, NG - 1, (NG - 1) // SLOTS)

            def x_plus_beta(b):
                pool.wait_ge(xt_in[b % TB], 16 * (b // TB + 1))
                nc.gpsimd.tensor_tensor(xt[b % TB][:], xt[b % TB][:], betaB[:], ALU.add).then_inc(xb_ready, 1)

            pool.wait_ge(late_in, 48)
            for b in range(TB):
                x_plus_beta(b)
            for b in range(NT + 1):
                if b < NT:
                    pool.wait_ge(ve1_ready, b + 1)
                    nc.gpsimd.tensor_tensor(rs[:, b:b + 1], ve[:, b:b + 1], mhalf[:, 0:1], ALU.pow).then_inc(rs1_ready, 1)
                if b >= 1:
                    pool.wait_ge(ve2_ready, b)
                    nc.gpsimd.tensor_tensor(rs2[:, b - 1:b], ve2[:, b - 1:b], mhalf[:, 0:1], ALU.pow).then_inc(rs2_ready, 1)
                if b >= 1 and b - 1 + TB < NT:
                    x_plus_beta(b - 1 + TB)
            with pool.Fori(0, NT) as b:
                pool.wait_ge(h1_ready, b + 1)
                nc.gpsimd.tensor_tensor(U[:, bass.ds(b, 1), :], U[:, bass.ds(b, 1), :], b2B[:].rearrange("p (a d) -> p a d", a=1), ALU.add).then_inc(res_step, 1)
                pool.wait_ge(res_step, 2 * b + 1)
                nc.gpsimd.tensor_tensor(U[:, bass.ds(b, 1), :], U[:, bass.ds(b, 1), :], H[:, bass.ds(b, 1), :], ALU.add).then_inc(res_step, 1)

        @block.scalar
        def _(act):
            for k in range(2 * FC):
                act.wait_ge(wuT_mm, k + 1)
                nc.scalar.copy(WuT[:, k, :], ps[:, 6 + k % 2, :]).then_inc(wuT_done, 1)
            act.wait_ge(nb_ready, 1)
            with act.Fori(0, NT) as b:
                nc.scalar.activation(H[:, bass.ds(b, 1), :], H[:, bass.ds(b, 1), :], ACT.Relu, bias=nb[:, bass.ds(b, 1)],
                                     scale=rs[:, bass.ds(b, 1)]).then_inc(h0_ready, 1)
            for k in range(FC):
                act.wait_ge(ct_mm, k + 1)
                nc.scalar.copy(CT[:, k, :], ps[:, 4 + k % 2, :]).then_inc(ct_done, 1)
            act.wait_ge(ct_mm, FC + 1)
            nc.scalar.copy(cbB[:], ps[:, 4, :]).then_inc(ct_done, 1)

            def high_parts(s, turn):
                act.wait_ge(ea_in[s], 16 * (turn + 1))
                nc.scalar.copy(hi[s][:], ea[s][:, 2:4, :]).then_inc(hi_ready, 1)

            with act.Fori(0, (NG - 1) // SLOTS) as i:
                for s in range(SLOTS):
                    high_parts(s, i)
            high_parts(0, (NG - 1) // SLOTS)

            act.wait_ge(summed, 1)
            for c in range(0, NT, 2):
                nc.scalar.copy(AF[:, c, :], A16[:, c, 0:NP]).then_inc(conv[0], 1)
            act.wait_ge(small_in, 64)
            nc.scalar.activation(eps1[:], epsC[:], ACT.Copy, bias=1.0).then_inc(h1T_done, 1)

            def gelu(b):
                act.wait_ge(t_ready, b + 1)
                nc.scalar.activation(tt[b % TB][:], tt[b % TB][:], ACT.Gelu).then_inc(g_ready, 1)

            def h1(b):
                act.wait_ge(nb2_ready, b + 1)
                nc.scalar.activation(H[:, b, :], U[:, b, :], ACT.Relu, bias=nb[:, b:b + 1], scale=rs2[:, b:b + 1]).then_inc(h1_ready, 1)

            def h1T(b):
                if b == 0:
                    act.wait_ge(c_mm, NT)
                    act.wait_ge(h1T_done, 1)
                act.wait_ge(h1T_mm, b + 1)
                nc.scalar.activation(aggT[:, :, b * P:(b + 1) * P], ps[:, 6 + b % 2, :].rearrange("p (f n) -> p f n", f=FC),
                                     ACT.Copy, scale=eps1[:, 0:1]).then_inc(h1T_done, 1)

            for b in range(NT + 2):
                if b < NT:
                    gelu(b)
                if b >= 2:
                    h1(b - 2)
            for b in range(NT):
                h1T(b)
            act.wait_ge(rst_mm, NQ)
            with act.Fori(0, NQ) as q:
                for k in range(KC):
                    act.wait_ge(hid_mm, q * KC + k + 1)
                    nc.scalar.activation(hid[:, k, bass.ds(q * QC, QC)], ps[:, k % 4, 0:QC], ACT.Relu,
                                         bias=b1C[:, k:k + 1]).then_inc(hid_done, 1)

        @block.vector
        def _(dve):
            V = nc.vector
            count = [0]

            def step(ins):
                count[0] += 1
                ins.then_inc(prep, 1)
                dve.wait_ge(prep, count[0])

            dve.wait_ge(consts, 6 + TB)
            V.tensor_scalar(ident[:], iotaF[:], pid[:, 0:1], None, ALU.is_equal).then_inc(ident_ready, 1)
            dve.wait_ge(idx_in, 64)
            G = slice(0, NG)

            def tiles(t):
                return t[G, :].rearrange("g (j p) -> g j p", j=SUB)

            step(V.tensor_copy(dst_f[G, :], dst_i[G, :]))
            step(V.tensor_reduce(m4[G, 0:SUB], tiles(dst_f), AX.X, ALU.min))
            step(V.tensor_reduce(m4[G, 4:5], m4[G, 0:SUB], AX.X, ALU.min))
            step(V.tensor_copy(offs[G, 0:SUB], m4[G, 0:SUB]))
            step(V.tensor_copy(wi[G, 0:1], m4[G, 4:5]))
            step(V.tensor_scalar(wi[G, 1:2], wi[G, 0:1], 6, None, ALU.logical_shift_right))
            step(V.tensor_copy(wf[G, 0:1], wi[G, 1:2]))
            step(V.tensor_scalar(wf[G, 1:2], wf[G, 0:1], float(NW - 1), None, ALU.min))
            step(V.tensor_copy(offs[G, 4:5], wf[G, 1:2]))
            step(V.tensor_scalar(wf[G, 2:3], wf[G, 1:2], float(HALF), None, ALU.mult))
            step(V.tensor_scalar(drel[G, :], dst_f[G, :], wf[G, 2:3], None, ALU.subtract))
            step(V.tensor_tensor(tiles(wrel), tiles(dst_f), m4[G, 0:SUB].rearrange("g (j a) -> g j a", a=1).broadcast_to([NG, SUB, P]), ALU.subtract))
            step(V.tensor_scalar(valid[G, :], dst_f[G, :], float(N), None, ALU.is_lt))
            step(V.scalar_tensor_tensor(bigE[G, :], drel[G, :], float(P), valid[G, :], ALU.is_ge, ALU.mult))
            step(V.scalar_tensor_tensor(bigA[G, :], wrel[G, :], float(W), valid[G, :], ALU.is_ge, ALU.mult))
            step(V.scalar_tensor_tensor(tmpf[G, :], bigE[G, :], 1.0, bigA[G, :], ALU.mult, ALU.add))
            step(V.tensor_reduce(m4[G, 5:6], tmpf[G, :], AX.X, ALU.add))
            step(V.tensor_copy(offs[G, 5:6], m4[G, 5:6]))
            assert count[0] == PREP_OFFS
            step(V.scalar_tensor_tensor(tmpf[G, :], dst_f[G, :], 1.0, bigE[G, :], ALU.add, ALU.mult))
            step(V.tensor_scalar(dE[G, :], tmpf[G, :], -1.0, None, ALU.add))
            step(V.scalar_tensor_tensor(tmpf[G, :], dst_f[G, :], 1.0, bigA[G, :], ALU.add, ALU.mult))
            step(V.tensor_scalar(dA[G, :], tmpf[G, :], -1.0, None, ALU.add))
            step(V.tensor_scalar(hi_i[G, :], src_i[G, :], 7, None, ALU.logical_shift_right))
            step(V.tensor_scalar(lo_i[G, :], src_i[G, :], P - 1, None, ALU.bitwise_and))
            step(V.tensor_copy(hi_f[G, :], hi_i[G, :]))
            step(V.tensor_copy(lo_f[G, :], lo_i[G, :]))
            step(V.scalar_tensor_tensor(key[G, :], hi_f[G, :], float(W), wrel[G, :], ALU.mult, ALU.add))
            step(V.tensor_scalar(tmpf[G, :], wrel[G, :], float(W), 4096.0, ALU.is_ge, ALU.mult))
            step(V.tensor_tensor(key[G, :], key[G, :], tmpf[G, :], ALU.add))
            assert count[0] == PREP_KEYS
            for q, name in enumerate(("drel", "key", "lo", "dE", "dA", "hi")):
                dve.wait_ge(idxT_mm, q + 1)
                V.tensor_copy(idxT[name][:, :, 0:NG], ps[:, q, 0:SUB * GP].rearrange("p (j g) -> p j g", j=SUB)[:, :, 0:NG]).then_inc(idxT_done, 1)
            dve.wait_ge(offs_in, 16)
            step(V.tensor_reduce(nunc_f[0:1, 0:1], offrow[0:1, :].rearrange("a (g k) -> a k g", k=8)[:, 5, :], AX.X, ALU.add))
            step(V.tensor_copy(nunc[0:1, 0:1], nunc_f[0:1, 0:1]))
            dve.wait_ge(idxT_done, 6)
            step(V.memset(A16[:].bitcast(I32), 0))
            assert count[0] == PREP_ALL

            dve.wait_ge(x_in, 32)
            with dve.Fori(0, NT) as b:
                V.bn_stats(stats[:, bass.ds(b, 1), :], H[:, bass.ds(b, 1), :]).then_inc(ln0, 1)
            dve.wait_ge(ln0, NT)
            for b in range(NT):
                V.bn_aggr(mv[:, b, :], stats[:, b, :]).then_inc(ln0, 1)
            dve.wait_ge(ln0, 2 * NT)
            V.tensor_scalar(ve[:], mv[:, :, 1], EPS, None, ALU.add).then_inc(ve_ready, 1)
            dve.wait_ge(rs_ready, 1)
            V.scalar_tensor_tensor(nb[:], mv[:, :, 0], -1.0, rs[:], ALU.mult, ALU.mult).then_inc(nb_ready, 1)
            dve.wait_ge(small_in, 64)
            V.tensor_copy(bmB[:], bmC[:].rearrange("p (m a) -> p m a", a=1).broadcast_to([P, FC, P])).then_inc(bmB_done, 1)

            def hT(b):
                dve.wait_ge(hT_mm, b + 1)
                V.tensor_copy(U[:, b, :], ps[:, b % 2, :]).then_inc(hT_done, 1)

            def u1(b):
                dve.wait_ge(u1_mm, b + 1)
                V.tensor_tensor(U[:, b, :], ps[:, 2 + b % 2, :], buB[:], ALU.add).then_inc(u1_done, 1)

            for b in range(NT + 1):
                if b < NT:
                    hT(b)
                if b >= 1:
                    u1(b - 1)
            dve.wait_ge(a_zero, 1)
            dve.wait_ge(u1_done, NT)
            V.sem_inc(psum_free, SLOTS)

            def one_hots(s, n):
                dve.wait_ge(group_done, n + 1)
                for j in range(SUB):
                    V.tensor_scalar(oneS[s][:, j, :], iotaB[:], idxT["lo"][:, j, bass.ds(n, 1)], None, ALU.is_equal)
                    V.tensor_scalar(oneK[s][:, j, :], iotaB[:, 0:KW], idxT["key"][:, j, bass.ds(n, 1)], None, ALU.is_equal)
                    last = V.tensor_scalar(oneD[s][:, j, :], iotaF[:], idxT["drel"][:, j, bass.ds(n, 1)], None, ALU.is_equal)
                last.then_inc(hot_ready, 1)

            def add_up(s, n):
                first = [dve.value_load(offrow[0:1, bass.ds(n * 8 + j, 1)], min_val=0, max_val=NP - 1) for j in range(SUB)]
                window = dve.value_load(offrow[0:1, bass.ds(n * 8 + 4, 1)], min_val=0, max_val=NW - 1)
                dve.wait_ge(group_done, n + SLOTS + 1)
                for j in range(SUB):
                    dve.wait_ge(add_step, n * (SUB + 1) + j + 1)
                    V.tensor_tensor(A16[:, :, bass.ds(first[j], W)], ps[:, 3 + s, j * KW:(j + 1) * KW].rearrange("p (h w) -> p h w", w=W),
                                    A16[:, :, bass.ds(first[j], W)], ALU.add).then_inc(add_step, 1)
                V.tensor_tensor(SW[:, bass.ds(window, 1), :], ps[:, s, :].rearrange("p (a d) -> p a d", a=1),
                                SW[:, bass.ds(window, 1), :], ALU.add).then_inc(add_step, 1)
                dve.wait_ge(add_step, (n + 1) * (SUB + 1) + 1)
                V.sem_inc(psum_free, 1)

            V.sem_inc(add_step, 1)
            one_hots(0, 0)
            with dve.Fori(0, (NG - 1) // SLOTS) as i:
                for s in range(SLOTS):
                    one_hots((s + 1) % SLOTS, i * SLOTS + s + 1)
                    add_up(s, i * SLOTS + s)
            add_up(0, NG - 1)

            uncovered = dve.value_load(nunc[0:1, 0:1], min_val=0, max_val=2 * E)
            with dve.If(uncovered > 0):
                with dve.Fori(0, NT) as b:
                    with dve.Fori(0, NG) as g:
                        dve.wait_ge(gen_mm, b * NG + g + 1)
                        for j in range(SUB):
                            last = V.tensor_scalar(oneD[0][:, j, :], iotaF[:], idxT["dE"][:, j, bass.ds(g, 1)], None, ALU.is_equal)
                        last.then_inc(gen_hot, 1)
                        dve.wait_ge(gen_mm, b * NG + g + 2)
                        V.tensor_tensor(SW[:, bass.ds(b * (P // HALF), 1), :], ps[:, 0, :].rearrange("p (a d) -> p a d", a=1),
                                        SW[:, bass.ds(b * (P // HALF), 1), :], ALU.add).then_inc(gen_add, 1)
                        dve.wait_ge(gen_add, b * NG + g + 1)
                    V.tensor_scalar(idxT["dE"][:, :, 0:NG], idxT["dE"][:, :, 0:NG], float(-P), None, ALU.add).then_inc(gen_step, 1)
                    dve.wait_ge(gen_step, b + 1)
                with dve.Fori(0, NT) as b:
                    with dve.Fori(0, HB) as h:
                        V.tensor_scalar(idxT["key"][:, :, 0:NG], idxT["hi"][:, :, 0:NG], 0.0, None, ALU.is_equal).then_inc(gen_step, 1)
                        with dve.Fori(0, NG) as g:
                            dve.wait_ge(gen_step, b * (2 * HB + 2) + h * 2 + NT + 1)
                            dve.wait_ge(gen_mm, NT * NG + (b * HB + h) * NG + g + 1)
                            for j in range(SUB):
                                V.tensor_scalar(oneS[0][:, j, :], iotaB[:], idxT["lo"][:, j, bass.ds(g, 1)], None, ALU.is_equal)
                                last = V.tensor_scalar(oneS[1][:, j, :], iotaB[:], idxT["dA"][:, j, bass.ds(g, 1)],
                                                       idxT["key"][:, j, bass.ds(g, 1)], ALU.is_equal, ALU.mult)
                            last.then_inc(gen_hot, 1)
                            dve.wait_ge(gen_mm, NT * NG + (b * HB + h) * NG + g + 2)
                            V.tensor_tensor(A16[:, bass.ds(h, 1), bass.ds(b * P, P)], ps[:, 0, 0:P].rearrange("p (a d) -> p a d", a=1),
                                            A16[:, bass.ds(h, 1), bass.ds(b * P, P)], ALU.add).then_inc(gen_add, 1)
                            dve.wait_ge(gen_add, NT * NG + (b * HB + h) * NG + g + 1)
                        V.tensor_scalar(idxT["hi"][:, :, 0:NG], idxT["hi"][:, :, 0:NG], -1.0, None, ALU.add).then_inc(gen_step, 1)
                        dve.wait_ge(gen_step, b * (2 * HB + 2) + h * 2 + NT + 2)
                    V.tensor_scalar(idxT["hi"][:, :, 0:NG], idxT["hi"][:, :, 0:NG], float(HB), None, ALU.add).then_inc(gen_step, 1)
                    V.tensor_scalar(idxT["dA"][:, :, 0:NG], idxT["dA"][:, :, 0:NG], float(-P), None, ALU.add).then_inc(gen_step, 1)
                    dve.wait_ge(gen_step, (b + 1) * (2 * HB + 2) + NT)
                V.engine_nop() if hasattr(V, "engine_nop") else V.nop()
            V.nop().then_inc(summed, 1)

            dve.wait_ge(summed, 1)
            for c in range(1, NT, 2):
                V.tensor_copy(AF[:, c, :], A16[:, c, 0:NP]).then_inc(conv[1], 1)
            V.tensor_reduce(Dsum[:], A16[:, :, 0:NP].rearrange("p h n -> p n h"), AX.X, ALU.add).then_inc(dsum_ready, 1)
            dve.wait_ge(dsum_ready, 1)
            dve.wait_ge(conv[0], NT // 2)

            for n, w in enumerate(list(range(0, NW, 2)) + list(range(1, NW, 2))):
                part = aggT[:, :, w * HALF:w * HALF + P]
                tp = ps[:, 4 + n % 2, :].rearrange("p (f n) -> p f n", f=FC)
                dve.wait_ge(win_mm, n + 1)
                if w % 2 == 0:
                    V.tensor_copy(part, tp).then_inc(win_add, 1)
                else:
                    if w == 1:
                        dve.wait_ge(win_add, (NW + 1) // 2)
                    V.tensor_tensor(part, tp, part, ALU.add).then_inc(win_add, 1)
            dve.wait_ge(win_add, NW)
            dve.wait_ge(deg_mm, 1)
            V.tensor_scalar(degs[:], ps[:, 6, 0:NT], 1.0, None, ALU.max).then_inc(deg_step, 1)
            V.tensor_scalar(has[:], ps[:, 6, 0:NT], 1.0, None, ALU.min).then_inc(deg_step, 1)
            dve.wait_ge(deg_step, 2)
            V.reciprocal(rdeg[:], degs[:]).then_inc(deg_step, 1)
            dve.wait_ge(ct_done, FC + 1)
            for b in range(NT):
                V.scalar_tensor_tensor(U[:, b, :], cbB[:], has[:, b:b + 1], U[:, b, :], ALU.mult, ALU.add).then_inc(deg_step, 1)
            dve.wait_ge(deg_step, 3 + NT)
            for q in range(NQ):
                dve.wait_ge(agg_mm, q + 1)
                part = aggT[:, :, q * QC:(q + 1) * QC]
                V.tensor_tensor(part, ps[:, (q % 2) * 4:(q % 2) * 4 + FC, 0:QC], part, ALU.add).then_inc(agg_done, 1)

            o_count = [0]

            def ostep(ins):
                o_count[0] += 1
                ins.then_inc(o_step, 1)
                dve.wait_ge(o_step, o_count[0])

            def update(b):
                dve.wait_ge(c_mm, b + 1)
                V.scalar_tensor_tensor(tt[b % TB][:], ps[:, b % 2, :], rdeg[:, b:b + 1], U[:, b, :], ALU.mult, ALU.add).then_inc(t_ready, 1)

            def norm(b):
                t = tt[b % TB]
                dve.wait_ge(g_ready, b + 1)
                ostep(V.tensor_tensor(t[:], t[:], H[:, b, :], ALU.add))
                ostep(V.bn_stats(stats[:, b, :], t[:]))
                ostep(V.bn_aggr(mv[:, b, :], stats[:, b, :]))
                V.tensor_scalar(ve[:, b:b + 1], mv[:, b, 1:2], EPS, None, ALU.add).then_inc(ve1_ready, 1)

            def residual(b):
                t = tt[b % TB]
                dve.wait_ge(rs1_ready, b + 1)
                ostep(V.tensor_scalar(t[:], t[:], mv[:, b, 0:1], rs[:, b:b + 1], ALU.subtract, ALU.mult))
                ostep(V.tensor_tensor(t[:], t[:], gammaB[:], ALU.mult))
                dve.wait_ge(xb_ready, b + 1)
                V.tensor_tensor(U[:, b, :], t[:], xt[b % TB][:], ALU.add).then_inc(x1_ready, 1)
                dve.wait_ge(x1_ready, b + 1)
                ostep(V.bn_stats(stats[:, b, :], U[:, b, :]))
                ostep(V.bn_aggr(mv2[:, b, :], stats[:, b, :]))
                V.tensor_scalar(ve2[:, b:b + 1], mv2[:, b, 1:2], EPS, None, ALU.add).then_inc(ve2_ready, 1)

            def shift(b):
                dve.wait_ge(rs2_ready, b + 1)
                V.scalar_tensor_tensor(nb[:, b:b + 1], mv2[:, b, 0:1], -1.0, rs2[:, b:b + 1], ALU.mult, ALU.mult).then_inc(nb2_ready, 1)

            dve.wait_ge(late_in, 48)
            for b in range(NT + 2):
                if b < NT:
                    update(b)
                if 1 <= b <= NT:
                    norm(b - 1)
                if b >= 2:
                    shift(b - 2)
                if 1 <= b <= NT:
                    residual(b - 1)

            for q in range(NQ):
                dve.wait_ge(rst_mm, q + 1)
                if q == 0:
                    dve.wait_ge(h1T_done, NT + 1)
                part = aggT[:, :, q * QC:(q + 1) * QC]
                V.tensor_tensor(part, ps[:, (q % 2) * 4:(q % 2) * 4 + FC, 0:QC], part, ALU.add).then_inc(rst_done, 1)
            for b in range(NT):
                dve.wait_ge(y_mm, b + 1)
                dve.wait_ge(res_step, 2 * b + 2)
                V.tensor_tensor(U[:, b, :], ps[:, 4 + b % 2, :], U[:, b, :], ALU.add).then_inc(y_done, 1)

        @block.tensor
        def _(pe):
            T = nc.tensor
            pe.wait_ge(ident_ready, 1)
            for q, (name, mine) in enumerate((("drel", drel), ("key", key), ("lo", lo_f), ("dE", dE), ("dA", dA), ("hi", hi_f))):
                if q == 0:
                    pe.wait_ge(prep, PREP_KEYS)
                for j in range(SUB):
                    cols = slice(j, GE, SUB) if name in ("drel", "dE") else slice(j * P, (j + 1) * P)
                    last = T.transpose(ps[:, q, j * GP:j * GP + NG], mine[0:NG, cols], ident[0:NG, 0:NG])
                last.then_inc(idxT_mm, 1)
            pe.wait_ge(wu_in, 16)
            for k in range(2 * FC):
                if k >= 2:
                    pe.wait_ge(wuT_done, k - 1)
                for o in range(FC):
                    last = T.transpose(ps[:, 6 + k % 2, o * P:(o + 1) * P], WuN[:, o, k * P:(k + 1) * P], ident[:])
                last.then_inc(wuT_mm, 1)
            pe.wait_ge(wuT_done, 2 * FC)
            pe.wait_ge(idxT_done, 6)

            def transpose_h0(b):
                pe.wait_ge(h0_ready, b + 1)
                if b >= 2:
                    pe.wait_ge(hT_done, b - 1)
                for f in range(FC):
                    last = T.transpose(ps[:, b % 2, f * P:(f + 1) * P], H[:, b, f * P:(f + 1) * P], ident[:])
                last.then_inc(hT_mm, 1)

            def first_half(b):
                pe.wait_ge(hT_done, b + 1)
                if b >= 2:
                    pe.wait_ge(u1_done, b - 1)
                for f in range(FC):
                    last = T.matmul(ps[:, 2 + b % 2, :], U[:, b, f * P:(f + 1) * P], WuT[:, f, :], start=f == 0, stop=f == FC - 1)
                last.then_inc(u1_mm, 1)

            pe.wait_ge(wm_in, 16)
            for k in range(FC):
                if k >= 2:
                    pe.wait_ge(ct_done, k - 1)
                for m in range(FC):
                    last = T.matmul(ps[:, 4 + k % 2, :], WmN[:, m, k * P:(k + 1) * P], WuT[:, FC + m, :], start=m == 0, stop=m == FC - 1)
                last.then_inc(ct_mm, 1)
            pe.wait_ge(bmB_done, 1)
            pe.wait_ge(ct_done, FC - 1)
            for m in range(FC):
                last = T.matmul(ps[:, 4, :], bmB[:, m, :], WuT[:, FC + m, :], start=m == 0, stop=m == FC - 1)
            last.then_inc(ct_mm, 1)
            for b in range(NT + 1):
                if b < NT:
                    transpose_h0(b)
                if b >= 1:
                    first_half(b - 1)
            pe.wait_ge(u1_mm, NT)
            pe.wait_ge(ct_done, FC + 1)
            T.sem_inc(group_done, SLOTS)

            def group(s, n, turn):
                pe.wait_ge(psum_free, n + 1)
                pe.wait_ge(hot_ready, n + 1)
                for j in range(SUB):
                    T.matmul(ps[:, 3 + s, j * KW:(j + 1) * KW], oneS[s][:, j, :], oneK[s][:, j, :], start=True, stop=True)
                pe.wait_ge(ea_in[s], 16 * (turn + 1))
                for j in range(2):
                    T.matmul(ps[:, s, :], oneD[s][:, j, :].bitcast(F32), ea[s][:, j, :], start=j == 0, stop=False)
                pe.wait_ge(hi_ready, n + 1)
                for j in range(2):
                    T.matmul(ps[:, s, :], oneD[s][:, 2 + j, :], hi[s][:, j, :], start=False, stop=False)
                pe.wait_ge(lo_ready, n + 1)
                for j in range(2):
                    last = T.matmul(ps[:, s, :], oneD[s][:, 2 + j, :], lo[s][:, j, :], start=False, stop=j == 1)
                last.then_inc(group_done, 1)

            with pe.Fori(0, (NG - 1) // SLOTS) as i:
                for s in range(SLOTS):
                    group(s, i * SLOTS + s, i)
            group(0, NG - 1, (NG - 1) // SLOTS)

            pe.wait_ge(prep, PREP_ALL)
            uncovered = pe.value_load(nunc[0:1, 0:1], min_val=0, max_val=2 * E)
            with pe.If(uncovered > 0):
                pe.wait_ge(psum_free, NG + SLOTS)
                T.sem_inc(gen_mm, 1)
                with pe.Fori(0, NT * NG) as n:
                    pe.wait_ge(gen_ea_in, 16 * n + 16)
                    pe.wait_ge(gen_hot, n + 1)
                    for j in range(SUB):
                        last = T.matmul(ps[:, 0, :], oneD[0][:, j, :].bitcast(F32), ea[0][:, j, :], start=j == 0, stop=j == SUB - 1)
                    last.then_inc(gen_mm, 1)
                with pe.Fori(0, NT * HB * NG) as n:
                    pe.wait_ge(gen_hot, n + NT * NG + 1)
                    for j in range(SUB):
                        last = T.matmul(ps[:, 0, 0:P], oneS[0][:, j, :], oneS[1][:, j, :], start=j == 0, stop=j == SUB - 1)
                    last.then_inc(gen_mm, 1)
                pe.nop()

            pe.wait_ge(summed, 1)
            for n, w in enumerate(list(range(0, NW, 2)) + list(range(1, NW, 2))):
                if n >= 2:
                    pe.wait_ge(win_add, n - 1)
                for f in range(FC):
                    last = T.transpose(ps[:, 4 + n % 2, f * P:(f + 1) * P], SW[:, w, f * P:(f + 1) * P], ident[:])
                last.then_inc(win_mm, 1)
            pe.wait_ge(dsum_ready, 1)
            for b in range(NT):
                last = T.matmul(ps[:, 6, b:b + 1], Dsum[:, b * P:(b + 1) * P], onesF[:, 0:1], start=True, stop=True)
            last.then_inc(deg_mm, 1)

            def times_A(base, q):
                for c in range(NT):
                    if base == 0:
                        for e in range(2):
                            if c % 2 == e:
                                pe.wait_ge(conv[e], c // 2 + 1)
                    for f in range(FC):
                        last = T.matmul(ps[:, (q % 2) * 4 + f, 0:QC], H[:, c, f * P:(f + 1) * P], AF[:, c, q * QC:(q + 1) * QC],
                                        start=c == 0, stop=c == NT - 1)
                last.then_inc(agg_mm if base == 0 else rst_mm, 1)

            for q in range(NQ):
                if q == 1:
                    pe.wait_ge(win_add, NW)
                    pe.wait_ge(deg_step, 2)
                if q >= 2:
                    pe.wait_ge(agg_done, q - 1)
                times_A(0, q)
            for b in range(NT):
                pe.wait_ge(agg_done, min(NQ, (b * P) // QC + 1))
                if b == 0:
                    pe.wait_ge(agg_done, NQ)
                if b >= 2:
                    pe.wait_ge(t_ready, b - 1)
                for f in range(FC):
                    last = T.matmul(ps[:, b % 2, :], aggT[:, f, b * P:(b + 1) * P], CT[:, f, :], start=f == 0, stop=f == FC - 1)
                last.then_inc(c_mm, 1)
            for b in range(NT):
                pe.wait_ge(h1_ready, b + 1)
                if b >= 2:
                    pe.wait_ge(h1T_done, b)
                for f in range(FC):
                    last = T.transpose(ps[:, 6 + b % 2, f * P:(f + 1) * P], H[:, b, f * P:(f + 1) * P], ident[:])
                last.then_inc(h1T_mm, 1)
            for q in range(NQ):
                if q == 0:
                    pe.wait_ge(t_ready, NT)
                if q == 1:
                    pe.wait_ge(h1T_done, NT + 1)
                if q >= 2:
                    pe.wait_ge(rst_done, q - 1)
                times_A(1, q)
            pe.wait_ge(w12_in, 32)
            pe.wait_ge(rst_done, NQ)
            T.sem_inc(hid_done, 4)
            with pe.Fori(0, NQ) as q:
                for k in range(KC):
                    pe.wait_ge(hid_done, q * KC + k + 1)
                    for f in range(FC):
                        last = T.matmul(ps[:, k % 4, 0:QC], W1s[:, f, k * P:(k + 1) * P], aggT[:, f, bass.ds(q * QC, QC)],
                                        start=f == 0, stop=f == FC - 1)
                    last.then_inc(hid_mm, 1)
            for b in range(NT):
                pe.wait_ge(hid_done, min(NQ, (b * P) // QC + 1) * KC + 4)
                if b >= 2:
                    pe.wait_ge(y_done, b - 1)
                for k in range(KC):
                    last = T.matmul(ps[:, 4 + b % 2, :], hid[:, k, b * P:(b + 1) * P], W2s[:, k, :], start=k == 0, stop=k == KC - 1)
                last.then_inc(y_mm, 1)


_INS = ['x', 'src', 'dst', 'edge_attr_512', 'L0_gnn_Wm', 'L0_gnn_bm', 'L0_gnn_Wu', 'L0_gnn_bu', 'L0_gnn_gamma',
        'L0_gnn_beta', 'L1_gnn_W1', 'L1_gnn_b1', 'L1_gnn_W2', 'L1_gnn_b2', 'L1_gnn_eps']
_OUTS = [((1250, 512), 'float32')]


def kernel(**inputs):
    import numpy as _np
    import concourse.bacc as _bacc
    from concourse import mybir as _mybir
    from concourse.bass_utils import run_bass_kernel_spmd as _run

    nc = _bacc.Bacc("TRN2", target_bir_lowering=False, num_devices=1)
    arrays, args = {}, []
    for name in _INS:
        a = _np.ascontiguousarray(inputs[name])
        arrays[f"in_{name}_dram"] = a
        args.append(nc.dram_tensor(f"in_{name}_dram", a.shape, _mybir.dt.from_np(a.dtype), kind="ExternalInput").ap())
    for i, (shape, dtype) in enumerate(_OUTS):
        dt = _mybir.dt.from_np(_np.dtype(dtype))
        args.append(nc.dram_tensor(f"out_{i}_dram", shape, dt, kind="ExternalOutput").ap())
    gnn_kernel(nc, *args)
    r = _run(nc, [arrays], core_ids=[0])
    return r.results[0]["out_0_dram"]
```

```python
from contextlib import ExitStack

import concourse.bass as bass
from concourse import mybir

F32 = mybir.dt.float32
F32R = mybir.dt.float32r
BF16 = mybir.dt.bfloat16
I32 = mybir.dt.int32
U16 = mybir.dt.uint16
ALU = mybir.AluOpType
ACT = mybir.ActivationFunctionType
AX = mybir.AxisListType

P = 128
SUB = 4
SLOTS = 4
HOTS = 2
SA = 3
W = 12
HALF = 64
EPS = 1e-5
COUNT_MAX = 4096
PREP_OFFS = 18
PREP_KEYS = 29
PREP_ALL = 31


def gnn_kernel(nc, x, src, dst, edge, Wm, bm, Wu, bu, gamma, beta, W1, b1, W2, b2, eps, out):
    N, D = x.shape
    E = edge.shape[0]
    HID = W1.shape[1]
    NT = -(-N // P)
    NP = NT * P
    TAIL = N - (NT - 1) * P
    FC = D // P
    KC = HID // P
    GE = SUB * P
    NG = -(-E // GE)
    ETAIL = E - (NG - 1) * GE
    GP = NG + 1
    HB = NT
    KW = HB * W
    NW = (NP - P) // HALF + 1
    AW = NP + W
    QC = 256
    NQ = NP // QC
    NCONV = NT
    TURNS = (NG - 1) // SLOTS
    assert ETAIL % SUB == 0 and D == GE and NQ == 5 and NG - TURNS * SLOTS == 3

    at = [-(-nc.sbuf_base // 64) * 64]

    def place(name, shape, dt, offset=None):
        size = mybir.dt.size(dt)
        for n in shape[1:]:
            size *= n
        if offset is None:
            offset = at[0]
            at[0] += -(-size // 32) * 32
        return nc.alloc_sbuf_tensor_at(name, shape, dt, offset=offset), offset

    X, x_at = place("X", [P, NT, D], F32)
    Hl, _ = place("Hl", [P, NT, D], F32R, x_at)
    Hh, _ = place("Hh", [P, NT, D], F32R)
    U, _ = place("U", [P, NT, D], F32)
    A16, a16_at = place("A16", [P, HB, AW], U16)
    SW, sw_at = place("SW", [P, NW, D], F32)
    CT, _ = place("CT", [P, FC, D], F32)
    stream_at = at[0]

    def size_of(shape, dt):
        size = mybir.dt.size(dt)
        for n in shape[1:]:
            size *= n
        return size

    ea = [place(f"ea{s}", [P, SUB, D], F32)[0] for s in range(SLOTS)]
    hots_at = at[0]
    hi, lo, oneD, oneS, oneK = [], [], [], [], []
    for s in range(HOTS):
        for lst, name, shape, dt in ((hi, "hi", [P, 2, D], F32R), (lo, "lo", [P, 2, D], F32R), (oneD, "oneD", [P, SUB, P], F32R),
                                     (oneS, "oneS", [P, SUB, P], BF16), (oneK, "oneK", [P, SUB, KW], BF16)):
            lst.append(place(f"{name}{s}", shape, dt)[0])
    hots1_at = hots_at + (at[0] - hots_at) // HOTS
    at[0] = max(at[0], stream_at + NT * NP * 4 + 3 * D * 4)
    WuN, _ = place("WuN", [P, FC, 2 * D], F32, stream_at)
    WuT, _ = place("WuT", [P, 2 * FC, D], F32, stream_at + 16384)
    WmN, _ = place("WmN", [P, FC, D], F32, hots1_at)
    bmB, _ = place("bmB", [P, FC, P], F32, hots1_at + 8192)
    AR, _ = place("AR", [P, NT, NP], F32R, stream_at)
    AF, _ = place("AF", [P, NT, NP], F32, stream_at)
    hid, _ = place("hid", [P, KC, NP], F32, stream_at)
    fold, _ = place("fold", [P, HB // 2, NP], U16, stream_at + 7 * NP * 4)
    spare = stream_at + NT * NP * 4
    gammaB, _ = place("gammaB", [P, D], F32, spare)
    betaB, _ = place("betaB", [P, D], F32, spare + 2048)
    b2B, _ = place("b2B", [P, D], F32, spare + 4096)
    aggT, _ = place("aggT", [P, FC, NP], F32, a16_at)
    W1s, _ = place("W1s", [P, FC, HID], F32, sw_at)
    W2s, _ = place("W2s", [P, KC, D], F32, sw_at + 16384)
    g_tmp = {}
    for n, name in enumerate(["dst_f", "bigE", "bigA", "valid", "drel", "wrel", "dE", "dA", "hi_f", "lo_f", "key", "tmp"]):
        g_tmp[name], _ = place("g_" + name, [P, GE], F32, a16_at + n * 2048)
    dst_f, bigE, bigA, valid, drel, wrel, dE, dA, hi_f, lo_f, key, tmpf = g_tmp.values()
    dst_i, _ = place("dst_i", [P, GE], I32, sw_at)
    src_i, _ = place("src_i", [P, GE], I32, sw_at + 2048)
    hi_i, _ = place("hi_i", [P, GE], I32, sw_at + 4096)
    lo_i, _ = place("lo_i", [P, GE], I32, sw_at + 6144)
    idx_at = -(-at[0] // 32) * 32
    idxT = {n: place("T_" + n, [P, SUB, GP], F32)[0] for n in ("drel", "key", "lo", "dE", "dA", "hi")}
    iotaF, _ = place("iotaF", [P, P], F32)
    iotaB, _ = place("iotaB", [P, P], BF16)
    ident, _ = place("ident", [P, P], F32)
    pid, _ = place("pid", [P, 1], F32)
    onesF, _ = place("onesF", [P, 1], F32)
    mhalf, _ = place("mhalf", [P, NT], F32)
    buB, _ = place("buB", [P, D], F32)
    cbB, _ = place("cbB", [P, D], F32)
    bmC, _ = place("bmC", [P, FC], F32)
    b1C, _ = place("b1C", [P, KC], F32)
    epsC, _ = place("epsC", [P, 1], F32)
    eps1, _ = place("eps1", [P, 1], F32)
    m4, _ = place("m4", [P, 8], F32)
    wf, _ = place("wf", [P, 4], F32)
    wi, _ = place("wi", [P, 2], I32)
    offs, _ = place("offs", [P, 8], U16)
    offrow, _ = place("offrow", [1, NG * 8], U16)
    square = [place(f"square{h}", [P, SA, P], F32)[0] for h in range(HOTS)]
    most, _ = place("most", [P, 1], F32)
    most1_f, _ = place("most1_f", [1, 1], F32)
    most1, _ = place("most1", [1, 1], I32)
    nunc_f, _ = place("nunc_f", [1, 2], F32)
    nunc, _ = place("nunc", [1, 2], I32)
    stats, _ = place("stats", [P, NT, 6], F32)
    mv, _ = place("mv", [P, NT, 2], F32)
    mv2, _ = place("mv2", [P, NT, 2], F32)
    ve, _ = place("ve", [P, NT], F32)
    ve2, _ = place("ve2", [P, NT], F32)
    rs, _ = place("rs", [P, NT], F32)
    rs2, _ = place("rs2", [P, NT], F32)
    nb, _ = place("nb", [P, NT], F32)
    degs, _ = place("degs", [P, NT], F32)
    rdeg, _ = place("rdeg", [P, NT], F32)
    has, _ = place("has", [P, NT], F32)
    TB = 3
    Dsum, _ = place("Dsum", [P, NP], F32, idx_at)
    tt = [place(f"tt{i}", [P, D], F32, idx_at + i * 2048)[0] for i in range(TB)]
    h0t = [place(f"h0t{i}", [P, D], F32, sw_at + 32768 + i * 2048)[0] for i in range(TB)]
    xt = [place(f"xt{i}", [P, D], F32, a16_at + 20480 + i * 2048)[0] for i in range(2)] + [place("xt2", [P, D], F32)[0]]
    assert at[0] <= nc.sbuf_usable_end, at[0] - nc.sbuf_usable_end

    ctx = ExitStack()
    with ctx:
        ps = ctx.enter_context(nc.psum_tensor("ps", [P, 8, 512], F32))

        def sem(name):
            return ctx.enter_context(nc.semaphore(name))

        pads_set = sem("pads_set")
        consts = sem("consts")
        idx_in = sem("idx_in")
        x_in = sem("x_in")
        wu_in = sem("wu_in")
        wm_in = sem("wm_in")
        small_in = sem("small_in")
        prep = sem("prep")
        ident_ready = sem("ident_ready")
        offs_in = sem("offs_in")
        a_zero = sem("a_zero")
        idxT_mm = sem("idxT_mm")
        idxT_done = sem("idxT_done")
        wuT_mm = sem("wuT_mm")
        wuT_done = sem("wuT_done")
        ln0 = sem("ln0")
        ve_ready = sem("ve_ready")
        rs_ready = sem("rs_ready")
        nb_ready = sem("nb_ready")
        h0_ready = sem("h0_ready")
        hT_mm = sem("hT_mm")
        hT_done = sem("hT_done")
        u1_mm = sem("u1_mm")
        u1_done = sem("u1_done")
        bmB_done = sem("bmB_done")
        ct_mm = sem("ct_mm")
        ct_done = sem("ct_done")
        group_done = sem("group_done")
        ea_in = [sem(f"ea_in{s}") for s in range(SLOTS)]
        hi_ready = sem("hi_ready")
        lo_ready = sem("lo_ready")
        hi0_ready = sem("hi0_ready")
        split0 = sem("split0")
        square_ready = sem("square_ready")
        hotA_ready = sem("hotA_ready")
        h0t_ready = sem("h0t_ready")
        hi1_ready = sem("hi1_ready")
        split1 = sem("split1")
        hot_ready = sem("hot_ready")
        add_step = sem("add_step")
        gen_ea_in = sem("gen_ea_in")
        gen_hot = sem("gen_hot")
        gen_mm = sem("gen_mm")
        gen_add = sem("gen_add")
        gen_step = sem("gen_step")
        summed = sem("summed")
        fold_step = sem("fold_step")
        most_mm = sem("most_mm")
        most_ready = sem("most_ready")
        conv = sem("conv")
        conv_exact = sem("conv_exact")
        dsum_ready = sem("dsum_ready")
        deg_mm = sem("deg_mm")
        deg_step = sem("deg_step")
        win_mm = sem("win_mm")
        win_add = sem("win_add")
        agg_mm = sem("agg_mm")
        agg_done = sem("agg_done")
        c_mm = sem("c_mm")
        t_ready = sem("t_ready")
        g_ready = sem("g_ready")
        o_step = sem("o_step")
        ve1_ready = sem("ve1_ready")
        rs1_ready = sem("rs1_ready")
        ve2_ready = sem("ve2_ready")
        rs2_ready = sem("rs2_ready")
        x1_ready = sem("x1_ready")
        nb2_ready = sem("nb2_ready")
        h1_ready = sem("h1_ready")
        late_in = sem("late_in")
        w12_in = sem("w12_in")
        xt_in = [sem(f"xt_in{i}") for i in range(TB)]
        xb_ready = sem("xb_ready")
        h1T_mm = sem("h1T_mm")
        h1T_done = sem("h1T_done")
        rst_mm = sem("rst_mm")
        rst_done = sem("rst_done")
        hid_mm = sem("hid_mm")
        hid_done = sem("hid_done")
        res_step = sem("res_step")
        y_mm = sem("y_mm")
        y_done = sem("y_done")
        stored = sem("stored")

        block = ctx.enter_context(nc.Block())

        edge_g = edge[0:(NG - 1) * GE, :].rearrange("(g p j) d -> g p j d", p=P, j=SUB)
        edge_tail = edge[(NG - 1) * GE:E, :].rearrange("(p j) d -> p j d", j=SUB)
        TP = ETAIL // SUB

        @block.sync
        def _(sp):
            sp.wait_ge(pads_set, 2)
            for t, a in ((dst_i, dst), (src_i, src)):
                sp.dma_start(t[0:NG - 1, :], a[0:(NG - 1) * GE].rearrange("(g e) -> g e", e=GE)).then_inc(idx_in, 16)
                sp.dma_start(t[NG - 1:NG, 0:ETAIL], a[(NG - 1) * GE:E].rearrange("(g e) -> g e", g=1)).then_inc(idx_in, 16)
            sp.dma_start(WuN[:], Wu.rearrange("(o p) i -> p o i", p=P)).then_inc(wu_in, 16)
            sp.wait_ge(pads_set, 3)
            sp.dma_start(X[:, 0:NT - 1, :], x[0:(NT - 1) * P, :].rearrange("(b p) d -> p b d", p=P)).then_inc(x_in, 16)
            sp.dma_start(X[0:TAIL, NT - 1, :], x[(NT - 1) * P:N, :]).then_inc(x_in, 16)
            sp.dma_start(WmN[:], Wm.rearrange("(m p) i -> p m i", p=P)).then_inc(wm_in, 16)
            sp.dma_start(buB[:], bu.rearrange("(a d) -> a d", a=1).broadcast_to([P, D])).then_inc(small_in, 16)
            sp.dma_start(bmC[:], bm.rearrange("(m p) -> p m", p=P), allow_slow_non_contiguous=True).then_inc(small_in, 16)
            sp.dma_start(b1C[:], b1.rearrange("(k p) -> p k", p=P), allow_slow_non_contiguous=True).then_inc(small_in, 16)
            sp.dma_start(epsC[:], eps.rearrange("(a d) -> a d", a=1).broadcast_to([P, 1])).then_inc(small_in, 16)
            sp.wait_ge(prep, PREP_OFFS)
            sp.dma_start(offrow[0:1, :], offs[0:NG, :]).then_inc(offs_in, 16)

            def load_group(s, n):
                sp.wait_ge(group_done, n + 1)
                sp.dma_start(ea[s][:], edge_g[bass.ds(n, 1)].rearrange("g p j d -> (g p) j d")).then_inc(ea_in[s], 16)

            with sp.Fori(0, TURNS) as i:
                for s in range(SLOTS):
                    load_group(s, i * SLOTS + s)
            load_group(0, NG - 3)
            load_group(1, NG - 2)
            sp.wait_ge(group_done, NG)
            sp.dma_start(ea[2][0:TP, :, :], edge_tail).then_inc(ea_in[2], 16)

            sp.wait_ge(group_done, NG + SLOTS)
            sp.wait_ge(prep, PREP_ALL)
            uncovered = sp.value_load(nunc[0:1, 0:1], min_val=0, max_val=2 * E)
            with sp.If(uncovered > 0):
                with sp.Fori(0, NT) as b:
                    with sp.Fori(0, NG - 1) as g:
                        sp.wait_ge(gen_mm, b * NG + g + 1)
                        sp.dma_start(ea[0][:], edge_g[bass.ds(g, 1)].rearrange("g p j d -> (g p) j d")).then_inc(gen_ea_in, 16)
                    sp.wait_ge(gen_mm, b * NG + NG)
                    sp.dma_start(ea[0][0:TP, :, :], edge_tail).then_inc(gen_ea_in, 16)
                sp.nop()

            sp.wait_ge(summed, 1)
            for t, a in ((gammaB, gamma), (betaB, beta), (b2B, b2)):
                sp.dma_start(t[:], a.rearrange("(a d) -> a d", a=1).broadcast_to([P, D])).then_inc(late_in, 16)

            def load_x(b):
                if b >= TB:
                    sp.wait_ge(x1_ready, b - TB + 1)
                elif b == 0:
                    sp.wait_ge(conv, NT)
                    sp.wait_ge(fold_step, 1)
                    sp.wait_ge(conv_exact, 1)
                if b < NT - 1:
                    sp.dma_start(xt[b % TB][:], x[b * P:(b + 1) * P, :]).then_inc(xt_in[b % TB], 16)
                else:
                    sp.dma_start(xt[b % TB][0:TAIL, :], x[b * P:N, :]).then_inc(xt_in[b % TB], 16)

            for b in range(TB):
                load_x(b)
            sp.wait_ge(win_mm, NW)
            sp.dma_start(W1s[:], W1.rearrange("(f p) h -> p f h", p=P)).then_inc(w12_in, 16)
            sp.dma_start(W2s[:], W2.rearrange("(k p) d -> p k d", p=P)).then_inc(w12_in, 16)
            for b in range(TB, NT):
                load_x(b)
            for b in range(NT):
                rows = P if b < NT - 1 else TAIL
                sp.wait_ge(y_done, b + 1)
                sp.dma_start(out[b * P:b * P + rows, :], U[0:rows, b, :]).then_inc(stored, 16)
            sp.wait_ge(stored, 16 * NT)

        @block.gpsimd
        def _(pool):
            nc.gpsimd.memset(dst_i[:], NP - 1).then_inc(pads_set, 1)
            nc.gpsimd.memset(src_i[:], 0).then_inc(pads_set, 1)
            nc.gpsimd.memset(X[:, NT - 1, :], 0.0).then_inc(pads_set, 1)
            nc.gpsimd.iota(iotaF[:], [[1, P]], base=0, channel_multiplier=0, allow_small_or_imprecise_dtypes=True).then_inc(consts, 1)
            nc.gpsimd.iota(pid[:], [[1, 1]], base=0, channel_multiplier=1, allow_small_or_imprecise_dtypes=True).then_inc(consts, 1)
            nc.gpsimd.iota(iotaB[:], [[1, P]], base=0, channel_multiplier=0, allow_small_or_imprecise_dtypes=True).then_inc(consts, 1)
            nc.gpsimd.memset(mhalf[:], -0.5).then_inc(consts, 1)
            nc.gpsimd.memset(onesF[:], 1.0).then_inc(consts, 1)
            nc.gpsimd.memset(offs[:], 0).then_inc(consts, 1)
            pool.wait_ge(consts, 6)
            pool.wait_ge(ve_ready, 1)
            nc.gpsimd.tensor_tensor(rs[:], ve[:], mhalf[:], ALU.pow).then_inc(rs_ready, 1)
            pool.wait_ge(prep, PREP_KEYS)
            nc.gpsimd.memset(SW[:], 0.0).then_inc(a_zero, 1)
            pool.wait_ge(idxT_mm, 6)
            nc.gpsimd.memset(A16[:].bitcast(I32), 0).then_inc(a_zero, 1)
            with pool.Fori(0, NT) as b:
                pool.wait_ge(hi0_ready, b + 1)
                pool.wait_ge(hT_mm, b + 1)
                nc.gpsimd.tensor_tensor(Hl[:, bass.ds(b, 1), :], X[:, bass.ds(b, 1), :], Hh[:, bass.ds(b, 1), :].bitcast(F32),
                                        ALU.subtract).then_inc(split0, 1)

            def low_parts(s, n, turn):
                h = s % HOTS
                pool.wait_ge(group_done, n + SLOTS - HOTS + 1)
                pool.wait_ge(ea_in[s], 16 * (turn + 1))
                pool.wait_ge(hi_ready, n + 1)
                nc.gpsimd.tensor_tensor(lo[h][:], ea[s][:, 2:4, :], hi[h][:].bitcast(F32), ALU.subtract).then_inc(lo_ready, 1)

            with pool.Fori(0, TURNS) as i:
                for s in range(SLOTS):
                    low_parts(s, i * SLOTS + s, i)
            for s in range(3):
                low_parts(s, TURNS * SLOTS + s, TURNS)

            pool.wait_ge(win_mm, NW)

            def ahead(b):
                pool.wait_ge(xt_in[b % TB], 16 * (b // TB + 1))
                nc.gpsimd.tensor_tensor(xt[b % TB][:], xt[b % TB][:], betaB[:], ALU.add).then_inc(xb_ready, 1)
                nc.gpsimd.tensor_tensor(h0t[b % TB][:], Hh[:, b, :].bitcast(F32), Hl[:, b, :].bitcast(F32), ALU.add).then_inc(h0t_ready, 1)

            pool.wait_ge(late_in, 48)
            for b in range(TB):
                ahead(b)
            for b in range(NT + 1):
                if b < NT:
                    pool.wait_ge(ve1_ready, b + 1)
                    nc.gpsimd.tensor_tensor(rs[:, b:b + 1], ve[:, b:b + 1], mhalf[:, 0:1], ALU.pow).then_inc(rs1_ready, 1)
                if b >= 1:
                    pool.wait_ge(ve2_ready, b)
                    nc.gpsimd.tensor_tensor(rs2[:, b - 1:b], ve2[:, b - 1:b], mhalf[:, 0:1], ALU.pow).then_inc(rs2_ready, 1)
                    if b - 1 + TB < NT:
                        ahead(b - 1 + TB)
            pool.wait_ge(h1_ready, NT)
            pool.wait_ge(split1, NT)
            with pool.Fori(0, NT) as b:
                t = U[:, bass.ds(b, 1), :]
                nc.gpsimd.tensor_tensor(t, t, b2B[:].rearrange("p (a d) -> p a d", a=1), ALU.add).then_inc(res_step, 1)
                pool.wait_ge(res_step, b * 3 + 1)
                nc.gpsimd.tensor_tensor(t, t, Hh[:, bass.ds(b, 1), :].bitcast(F32), ALU.add).then_inc(res_step, 1)
                pool.wait_ge(res_step, b * 3 + 2)
                nc.gpsimd.tensor_tensor(t, t, Hl[:, bass.ds(b, 1), :].bitcast(F32), ALU.add).then_inc(res_step, 1)

        @block.scalar
        def _(act):
            for k in range(2 * FC):
                act.wait_ge(wuT_mm, k + 1)
                nc.scalar.copy(WuT[:, k, :], ps[:, 6 + k % 2, :]).then_inc(wuT_done, 1)
            for k in range(FC):
                act.wait_ge(ct_mm, k + 1)
                nc.scalar.copy(CT[:, k, :], ps[:, 4 + k % 2, :]).then_inc(ct_done, 1)
            act.wait_ge(ct_mm, FC + 1)
            nc.scalar.copy(cbB[:], ps[:, 4, :]).then_inc(ct_done, 1)
            act.wait_ge(nb_ready, 1)
            for b in range(NT + 1):
                if b < NT:
                    nc.scalar.activation(X[:, b, :], X[:, b, :], ACT.Relu, bias=nb[:, b:b + 1], scale=rs[:, b:b + 1]).then_inc(h0_ready, 1)
                if b >= 1:
                    act.wait_ge(h0_ready, b)
                    nc.scalar.copy(Hh[:, b - 1, :], X[:, b - 1, :]).then_inc(hi0_ready, 1)

            def high_parts(s, n, turn):
                h = s % HOTS
                act.wait_ge(group_done, n + SLOTS - HOTS + 1)
                for j in range(SA):
                    ins = nc.scalar.activation(square[h][:, j, :], iotaF[:], ACT.Square, bias=idxT["lo"][:, j, bass.ds(n, 1)], scale=-1.0)
                ins.then_inc(square_ready, 1)
                act.wait_ge(ea_in[s], 16 * (turn + 1))
                nc.scalar.copy(hi[h][:], ea[s][:, 2:4, :]).then_inc(hi_ready, 1)
                act.wait_ge(square_ready, n + 1)
                nc.scalar.activation(oneS[h][:, 0:SA, :], square[h][:], ACT.Relu, bias=onesF[:, 0:1], scale=-1.0).then_inc(hotA_ready, 1)

            act.wait_ge(idxT_done, 6)
            with act.Fori(0, TURNS) as i:
                for s in range(SLOTS):
                    high_parts(s, i * SLOTS + s, i)
            for s in range(3):
                high_parts(s, TURNS * SLOTS + s, TURNS)

            act.wait_ge(summed, 1)
            for c in range(NT):
                if c == 7:
                    act.wait_ge(dsum_ready, 1)
                nc.scalar.copy(AR[:, c, :], A16[:, c, 0:NP]).then_inc(conv, 1)
            act.wait_ge(most_ready, 2)
            large = act.value_load(most1[0:1, 0:1], min_val=0, max_val=E + P)
            act.wait_ge(conv, NT)
            with act.If(large > COUNT_MAX):
                for c in range(NT):
                    ins = nc.scalar.copy(AF[:, c, :], A16[:, c, 0:NP])
                ins.then_inc(conv_exact, 1)
            with act.Else():
                nc.scalar.sem_inc(conv_exact, 1)
            act.wait_ge(small_in, 64)
            nc.scalar.activation(eps1[:], epsC[:], ACT.Copy, bias=1.0).then_inc(h1T_done, 1)

            def gelu(b):
                act.wait_ge(t_ready, b + 1)
                nc.scalar.activation(tt[b % TB][:], tt[b % TB][:], ACT.Gelu).then_inc(g_ready, 1)

            def h1(b):
                act.wait_ge(nb2_ready, b + 1)
                act.wait_ge(h0t_ready, b + 1)
                nc.scalar.activation(X[:, b, :], U[:, b, :], ACT.Relu, bias=nb[:, b:b + 1], scale=rs2[:, b:b + 1]).then_inc(h1_ready, 1)

            def h1_high(b):
                act.wait_ge(h1_ready, b + 1)
                nc.scalar.copy(Hh[:, b, :], X[:, b, :]).then_inc(hi1_ready, 1)

            def h1T(b):
                act.wait_ge(h1T_mm, b + 1)
                act.wait_ge(c_mm, b + 1)
                nc.scalar.activation(aggT[:, :, b * P:(b + 1) * P], ps[:, 6 + b % 2, :].rearrange("p (f n) -> p f n", f=FC),
                                     ACT.Copy, scale=eps1[:, 0:1]).then_inc(h1T_done, 1)

            act.wait_ge(h1T_done, 1)
            for b in range(NT + 3):
                if b < NT:
                    gelu(b)
                if b >= 3:
                    h1(b - 3)
                    h1_high(b - 3)
                    h1T(b - 3)
            act.wait_ge(rst_mm, NQ)
            with act.Fori(0, NQ) as q:
                for k in range(KC):
                    act.wait_ge(hid_mm, q * KC + k + 1)
                    nc.scalar.activation(hid[:, k, bass.ds(q * QC, QC)], ps[:, k % 4, 0:QC], ACT.Relu,
                                         bias=b1C[:, k:k + 1]).then_inc(hid_done, 1)

        @block.vector
        def _(dve):
            V = nc.vector
            count = [0]

            def step(ins):
                count[0] += 1
                ins.then_inc(prep, 1)
                dve.wait_ge(prep, count[0])

            dve.wait_ge(consts, 6)
            V.tensor_scalar(ident[:], iotaF[:], pid[:, 0:1], None, ALU.is_equal).then_inc(ident_ready, 1)
            dve.wait_ge(idx_in, 64)
            G = slice(0, NG)

            def tiles(t):
                return t[G, :].rearrange("g (j p) -> g j p", j=SUB)

            step(V.tensor_copy(dst_f[G, :], dst_i[G, :]))
            step(V.tensor_reduce(m4[G, 0:SUB], tiles(dst_f), AX.X, ALU.min))
            step(V.tensor_reduce(m4[G, 4:5], m4[G, 0:SUB], AX.X, ALU.min))
            step(V.tensor_copy(offs[G, 0:SUB], m4[G, 0:SUB]))
            step(V.tensor_copy(wi[G, 0:1], m4[G, 4:5]))
            step(V.tensor_scalar(wi[G, 1:2], wi[G, 0:1], 6, None, ALU.logical_shift_right))
            step(V.tensor_copy(wf[G, 0:1], wi[G, 1:2]))
            step(V.tensor_scalar(wf[G, 1:2], wf[G, 0:1], float(NW - 1), None, ALU.min))
            step(V.tensor_copy(offs[G, 4:5], wf[G, 1:2]))
            step(V.tensor_scalar(wf[G, 2:3], wf[G, 1:2], float(HALF), None, ALU.mult))
            step(V.tensor_scalar(drel[G, :], dst_f[G, :], wf[G, 2:3], None, ALU.subtract))
            step(V.tensor_tensor(tiles(wrel), tiles(dst_f), m4[G, 0:SUB].rearrange("g (j a) -> g j a", a=1).broadcast_to([NG, SUB, P]), ALU.subtract))
            step(V.tensor_scalar(valid[G, :], dst_f[G, :], float(N), None, ALU.is_lt))
            step(V.scalar_tensor_tensor(bigE[G, :], drel[G, :], float(P), valid[G, :], ALU.is_ge, ALU.mult))
            step(V.scalar_tensor_tensor(bigA[G, :], wrel[G, :], float(W), valid[G, :], ALU.is_ge, ALU.mult))
            step(V.scalar_tensor_tensor(tmpf[G, :], bigE[G, :], 1.0, bigA[G, :], ALU.mult, ALU.add))
            step(V.tensor_reduce(m4[G, 5:6], tmpf[G, :], AX.X, ALU.add))
            step(V.tensor_copy(offs[G, 5:6], m4[G, 5:6]))
            assert count[0] == PREP_OFFS
            step(V.scalar_tensor_tensor(tmpf[G, :], dst_f[G, :], 1.0, bigE[G, :], ALU.add, ALU.mult))
            step(V.tensor_scalar(dE[G, :], tmpf[G, :], -1.0, None, ALU.add))
            step(V.scalar_tensor_tensor(tmpf[G, :], dst_f[G, :], 1.0, bigA[G, :], ALU.add, ALU.mult))
            step(V.tensor_scalar(dA[G, :], tmpf[G, :], -1.0, None, ALU.add))
            step(V.tensor_scalar(hi_i[G, :], src_i[G, :], 7, None, ALU.logical_shift_right))
            step(V.tensor_scalar(lo_i[G, :], src_i[G, :], P - 1, None, ALU.bitwise_and))
            step(V.tensor_copy(hi_f[G, :], hi_i[G, :]))
            step(V.tensor_copy(lo_f[G, :], lo_i[G, :]))
            step(V.scalar_tensor_tensor(key[G, :], hi_f[G, :], float(W), wrel[G, :], ALU.mult, ALU.add))
            step(V.tensor_scalar(tmpf[G, :], wrel[G, :], float(W), 4096.0, ALU.is_ge, ALU.mult))
            step(V.tensor_tensor(key[G, :], key[G, :], tmpf[G, :], ALU.add))
            assert count[0] == PREP_KEYS
            dve.wait_ge(x_in, 32)
            with dve.Fori(0, NT) as b:
                V.bn_stats(stats[:, bass.ds(b, 1), :], X[:, bass.ds(b, 1), :]).then_inc(ln0, 1)
            dve.wait_ge(ln0, NT)
            for b in range(NT):
                V.bn_aggr(mv[:, b, :], stats[:, b, :]).then_inc(ln0, 1)
            dve.wait_ge(ln0, 2 * NT)
            V.tensor_scalar(ve[:], mv[:, :, 1], EPS, None, ALU.add).then_inc(ve_ready, 1)
            dve.wait_ge(rs_ready, 1)
            V.scalar_tensor_tensor(nb[:], mv[:, :, 0], -1.0, rs[:], ALU.mult, ALU.mult).then_inc(nb_ready, 1)
            dve.wait_ge(small_in, 64)
            V.tensor_copy(bmB[:], bmC[:].rearrange("p (m a) -> p m a", a=1).broadcast_to([P, FC, P])).then_inc(bmB_done, 1)

            for q, name in enumerate(("drel", "key", "lo", "dE", "dA", "hi")):
                dve.wait_ge(idxT_mm, q + 1)
                V.tensor_copy(idxT[name][:, :, 0:NG], ps[:, q, 0:SUB * GP].rearrange("p (j g) -> p j g", j=SUB)[:, :, 0:NG]).then_inc(idxT_done, 1)
            dve.wait_ge(offs_in, 16)
            step(V.tensor_reduce(nunc_f[0:1, 0:1], offrow[0:1, :].rearrange("a (g k) -> a k g", k=8)[:, 5, :], AX.X, ALU.add))
            step(V.tensor_copy(nunc[0:1, 0:1], nunc_f[0:1, 0:1]))
            assert count[0] == PREP_ALL

            def hT(b):
                dve.wait_ge(hT_mm, b + 1)
                V.tensor_copy(U[:, b, :], ps[:, b % 2, :]).then_inc(hT_done, 1)

            def u1(b):
                dve.wait_ge(u1_mm, b + 1)
                V.tensor_tensor(U[:, b, :], ps[:, 2 + b % 2, :], buB[:], ALU.add).then_inc(u1_done, 1)

            for b in range(NT + 1):
                if b < NT:
                    hT(b)
                if b >= 1:
                    u1(b - 1)
            dve.wait_ge(a_zero, 2)
            dve.wait_ge(u1_done, NT)
            V.sem_inc(add_step, SLOTS * (SUB + 1))

            def one_hots_dst(s, n):
                n1 = idxT["drel"][:, :, bass.ds(n, 1)].broadcast_to([P, SUB, P])
                V.tensor_tensor(oneD[s % HOTS][:], iotaF[:].rearrange("p (a n) -> p a n", a=1).broadcast_to([P, SUB, P]), n1, ALU.is_equal)

            def one_hots_key(s, n):
                for j in range(SA, SUB):
                    V.tensor_scalar(oneS[s % HOTS][:, j, :], iotaB[:], idxT["lo"][:, j, bass.ds(n, 1)], None, ALU.is_equal)
                n1 = idxT["key"][:, :, bass.ds(n, 1)].broadcast_to([P, SUB, KW])
                V.tensor_tensor(oneK[s % HOTS][:], iotaF[:, 0:KW].rearrange("p (a n) -> p a n", a=1).broadcast_to([P, SUB, KW]), n1,
                                ALU.is_equal).then_inc(hot_ready, 1)

            def offsets(n):
                _, loaded = nc.values_load_multi_w_load_instructions(
                    offrow[0:1, bass.ds(n * 8, SUB + 1)], engines=(mybir.EngineType.DVE,), min_val=0, max_val=NP - 1,
                    skip_runtime_bounds_check_because="each is the least of indices of nodes, or a window")
                window = nc.s_assert_within(loaded[SUB], 0, NW - 1, skip_runtime_bounds_check_because="it was clamped to the last window")
                return loaded[0:SUB], window

            def add_up(s, n, at_cols, ahead, more=None):
                first, window = at_cols
                dve.wait_ge(group_done, n + SLOTS + 1)

                def add_counts(j):
                    cols = A16[:, :, bass.ds(first[j], W)]
                    dve.wait_ge(add_step, (n + SLOTS) * (SUB + 1) + j)
                    V.tensor_tensor(cols, ps[:, 4 + s, j * KW:(j + 1) * KW].rearrange("p (h w) -> p h w", w=W), cols, ALU.add).then_inc(add_step, 1)

                add_counts(0)
                if ahead:
                    one_hots_dst(s, n + HOTS)
                add_counts(1)
                if ahead:
                    one_hots_key(s, n + HOTS)
                add_counts(2)
                following = offsets(n + 1) if more else None
                add_counts(3)
                t = SW[:, bass.ds(window, 1), :]
                V.tensor_tensor(t, ps[:, s, :].rearrange("p (a d) -> p a d", a=1), t, ALU.add).then_inc(add_step, 1)
                return following

            for n in range(HOTS):
                one_hots_dst(n, n)
                one_hots_key(n, n)
            with dve.Fori(0, TURNS) as i:
                where = offsets(i * SLOTS)
                for s in range(SLOTS):
                    where = add_up(s, i * SLOTS + s, where, True, s < SLOTS - 1)
            where = offsets(NG - 3)
            where = add_up(0, NG - 3, where, True, True)
            where = add_up(1, NG - 2, where, False, True)
            add_up(2, NG - 1, where, False)
            dve.wait_ge(add_step, (NG + SLOTS) * (SUB + 1))

            uncovered = dve.value_load(nunc[0:1, 0:1], min_val=0, max_val=2 * E)
            with dve.If(uncovered > 0):
                with dve.Fori(0, NT) as b:
                    with dve.Fori(0, NG) as g:
                        dve.wait_ge(gen_mm, b * NG + g + 1)
                        for j in range(SUB):
                            last = V.tensor_scalar(oneD[0][:, j, :], iotaF[:], idxT["dE"][:, j, bass.ds(g, 1)], None, ALU.is_equal)
                        last.then_inc(gen_hot, 1)
                        dve.wait_ge(gen_mm, b * NG + g + 2)
                        V.tensor_tensor(SW[:, bass.ds(b * (P // HALF), 1), :], ps[:, 0, :].rearrange("p (a d) -> p a d", a=1),
                                        SW[:, bass.ds(b * (P // HALF), 1), :], ALU.add).then_inc(gen_add, 1)
                        dve.wait_ge(gen_add, b * NG + g + 1)
                    V.tensor_scalar(idxT["dE"][:, :, 0:NG], idxT["dE"][:, :, 0:NG], float(-P), None, ALU.add).then_inc(gen_step, 1)
                    dve.wait_ge(gen_step, b + 1)
                with dve.Fori(0, NT) as b:
                    with dve.Fori(0, HB) as h:
                        V.tensor_scalar(idxT["key"][:, :, 0:NG], idxT["hi"][:, :, 0:NG], 0.0, None, ALU.is_equal).then_inc(gen_step, 1)
                        with dve.Fori(0, NG) as g:
                            dve.wait_ge(gen_step, b * (2 * HB + 2) + h * 2 + NT + 1)
                            dve.wait_ge(gen_mm, NT * NG + (b * HB + h) * NG + g + 1)
                            for j in range(SUB):
                                V.tensor_scalar(oneS[0][:, j, :], iotaB[:], idxT["lo"][:, j, bass.ds(g, 1)], None, ALU.is_equal)
                                last = V.tensor_scalar(oneS[1][:, j, :], iotaB[:], idxT["dA"][:, j, bass.ds(g, 1)],
                                                       idxT["key"][:, j, bass.ds(g, 1)], ALU.is_equal, ALU.mult)
                            last.then_inc(gen_hot, 1)
                            dve.wait_ge(gen_mm, NT * NG + (b * HB + h) * NG + g + 2)
                            V.tensor_tensor(A16[:, bass.ds(h, 1), bass.ds(b * P, P)], ps[:, 0, 0:P].rearrange("p (a d) -> p a d", a=1),
                                            A16[:, bass.ds(h, 1), bass.ds(b * P, P)], ALU.add).then_inc(gen_add, 1)
                            dve.wait_ge(gen_add, NT * NG + (b * HB + h) * NG + g + 1)
                        V.tensor_scalar(idxT["hi"][:, :, 0:NG], idxT["hi"][:, :, 0:NG], -1.0, None, ALU.add).then_inc(gen_step, 1)
                        dve.wait_ge(gen_step, b * (2 * HB + 2) + h * 2 + NT + 2)
                    V.tensor_scalar(idxT["hi"][:, :, 0:NG], idxT["hi"][:, :, 0:NG], float(HB), None, ALU.add).then_inc(gen_step, 1)
                    V.tensor_scalar(idxT["dA"][:, :, 0:NG], idxT["dA"][:, :, 0:NG], float(-P), None, ALU.add).then_inc(gen_step, 1)
                    dve.wait_ge(gen_step, (b + 1) * (2 * HB + 2) + NT)
                V.engine_nop() if hasattr(V, "engine_nop") else V.nop()
            V.nop().then_inc(summed, 1)

            dve.wait_ge(summed, 1)
            f = fold
            V.tensor_tensor(f[:], A16[:, 0:5, 0:NP], A16[:, 5:10, 0:NP], ALU.add).then_inc(fold_step, 1)
            dve.wait_ge(fold_step, 1)
            V.tensor_tensor(f[:, 0:2, :], f[:, 0:2, :], f[:, 2:4, :], ALU.add).then_inc(fold_step, 1)
            dve.wait_ge(fold_step, 2)
            V.tensor_tensor(f[:, 0, :], f[:, 0, :], f[:, 1, :], ALU.add).then_inc(fold_step, 1)
            dve.wait_ge(fold_step, 3)
            V.tensor_tensor(Dsum[:], f[:, 0, :], f[:, 4, :], ALU.add).then_inc(dsum_ready, 1)
            dve.wait_ge(dsum_ready, 1)
            V.tensor_reduce(most[:], Dsum[:], AX.X, ALU.max).then_inc(fold_step, 1)
            dve.wait_ge(most_mm, 1)
            V.tensor_reduce(most1_f[0:1, 0:1], ps[0:1, 7, 0:P], AX.X, ALU.max).then_inc(most_ready, 1)
            dve.wait_ge(most_ready, 1)
            V.tensor_copy(most1[0:1, 0:1], most1_f[0:1, 0:1]).then_inc(most_ready, 1)
            dve.wait_ge(conv, NT)
            dve.wait_ge(conv_exact, 1)

            for n, w in enumerate(list(range(0, NW, 2)) + list(range(1, NW, 2))):
                part = aggT[:, :, w * HALF:w * HALF + P]
                tp = ps[:, 4 + n % 2, :].rearrange("p (f n) -> p f n", f=FC)
                dve.wait_ge(win_mm, n + 1)
                if w % 2 == 0:
                    V.tensor_copy(part, tp).then_inc(win_add, 1)
                else:
                    if w == 1:
                        dve.wait_ge(win_add, (NW + 1) // 2)
                    V.tensor_tensor(part, tp, part, ALU.add).then_inc(win_add, 1)
            dve.wait_ge(win_add, NW)
            dve.wait_ge(deg_mm, 1)
            V.tensor_scalar(degs[:], ps[:, 6, 0:NT], 1.0, None, ALU.max).then_inc(deg_step, 1)
            V.tensor_scalar(has[:], ps[:, 6, 0:NT], 1.0, None, ALU.min).then_inc(deg_step, 1)
            dve.wait_ge(deg_step, 2)
            V.reciprocal(rdeg[:], degs[:]).then_inc(deg_step, 1)
            dve.wait_ge(ct_done, FC + 1)
            for q in range(NQ):
                dve.wait_ge(agg_mm, q + 1)
                part = aggT[:, :, q * QC:(q + 1) * QC]
                V.tensor_tensor(part, ps[:, (q % 2) * 4:(q % 2) * 4 + FC, 0:QC], part, ALU.add).then_inc(agg_done, 1)
                for b in range(2 * q, 2 * q + 2):
                    V.scalar_tensor_tensor(U[:, b, :], cbB[:], has[:, b:b + 1], U[:, b, :], ALU.mult, ALU.add).then_inc(deg_step, 1)
            dve.wait_ge(deg_step, 3 + NT)

            o_count = [0]

            def ostep(ins):
                o_count[0] += 1
                ins.then_inc(o_step, 1)
                dve.wait_ge(o_step, o_count[0])

            def update(b):
                dve.wait_ge(c_mm, b + 1)
                V.scalar_tensor_tensor(tt[b % TB][:], ps[:, 4 + b % 2, :], rdeg[:, b:b + 1], U[:, b, :], ALU.mult, ALU.add).then_inc(t_ready, 1)

            def norm(b):
                t = tt[b % TB]
                dve.wait_ge(g_ready, b + 1)
                dve.wait_ge(h0t_ready, b + 1)
                ostep(V.tensor_tensor(t[:], t[:], h0t[b % TB][:], ALU.add))
                ostep(V.bn_stats(stats[:, b, :], t[:]))
                ostep(V.bn_aggr(mv[:, b, :], stats[:, b, :]))
                V.tensor_scalar(ve[:, b:b + 1], mv[:, b, 1:2], EPS, None, ALU.add).then_inc(ve1_ready, 1)

            def residual(b):
                t = tt[b % TB]
                ostep(V.scalar_tensor_tensor(t[:], t[:], mv[:, b, 0:1], gammaB[:], ALU.subtract, ALU.mult))
                dve.wait_ge(rs1_ready, b + 1)
                dve.wait_ge(xb_ready, b + 1)
                V.scalar_tensor_tensor(U[:, b, :], t[:], rs[:, b:b + 1], xt[b % TB][:], ALU.mult, ALU.add).then_inc(x1_ready, 1)
                dve.wait_ge(x1_ready, b + 1)
                ostep(V.bn_stats(stats[:, b, :], U[:, b, :]))
                ostep(V.bn_aggr(mv2[:, b, :], stats[:, b, :]))
                V.tensor_scalar(ve2[:, b:b + 1], mv2[:, b, 1:2], EPS, None, ALU.add).then_inc(ve2_ready, 1)

            def shift(b):
                dve.wait_ge(rs2_ready, b + 1)
                V.scalar_tensor_tensor(nb[:, b:b + 1], mv2[:, b, 0:1], -1.0, rs2[:, b:b + 1], ALU.mult, ALU.mult).then_inc(nb2_ready, 1)

            dve.wait_ge(late_in, 48)
            def low_h1(b):
                dve.wait_ge(hi1_ready, b + 1)
                dve.wait_ge(h1T_mm, b + 1)
                V.tensor_tensor(Hl[:, b, :], X[:, b, :], Hh[:, b, :].bitcast(F32), ALU.subtract).then_inc(split1, 1)

            for b in range(NT + 5):
                if b < NT:
                    update(b)
                if 1 <= b <= NT:
                    norm(b - 1)
                if 2 <= b <= NT + 1:
                    residual(b - 2)
                if 3 <= b <= NT + 2:
                    shift(b - 3)
                if b >= 5:
                    low_h1(b - 5)

            for q in range(NQ):
                dve.wait_ge(rst_mm, q + 1)
                if q == 0:
                    dve.wait_ge(h1T_done, NT + 1)
                part = aggT[:, :, q * QC:(q + 1) * QC]
                V.tensor_tensor(part, ps[:, (q % 2) * 4:(q % 2) * 4 + FC, 0:QC], part, ALU.add).then_inc(rst_done, 1)
            for b in range(NT):
                dve.wait_ge(y_mm, b + 1)
                dve.wait_ge(res_step, 3 * b + 3)
                V.tensor_tensor(U[:, b, :], ps[:, 4 + b % 2, :], U[:, b, :], ALU.add).then_inc(y_done, 1)

        @block.tensor
        def _(pe):
            T = nc.tensor
            pe.wait_ge(ident_ready, 1)
            pe.wait_ge(wu_in, 16)
            for k in range(2 * FC):
                if k >= 2:
                    pe.wait_ge(wuT_done, k - 1)
                for o in range(FC):
                    last = T.transpose(ps[:, 6 + k % 2, o * P:(o + 1) * P], WuN[:, o, k * P:(k + 1) * P], ident[:])
                last.then_inc(wuT_mm, 1)
            pe.wait_ge(wuT_done, 2 * FC)
            pe.wait_ge(wm_in, 16)
            for k in range(FC):
                if k >= 2:
                    pe.wait_ge(ct_done, k - 1)
                for m in range(FC):
                    last = T.matmul(ps[:, 4 + k % 2, :], WmN[:, m, k * P:(k + 1) * P], WuT[:, FC + m, :], start=m == 0, stop=m == FC - 1)
                last.then_inc(ct_mm, 1)
            pe.wait_ge(bmB_done, 1)
            pe.wait_ge(ct_done, FC - 1)
            for m in range(FC):
                last = T.matmul(ps[:, 4, :], bmB[:, m, :], WuT[:, FC + m, :], start=m == 0, stop=m == FC - 1)
            last.then_inc(ct_mm, 1)
            pe.wait_ge(ct_mm, FC + 1)
            T.sem_inc(group_done, 2)
            pe.wait_ge(ct_done, FC + 1)
            pe.wait_ge(prep, PREP_KEYS)
            for q, (name, mine) in enumerate((("drel", drel), ("key", key), ("lo", lo_f), ("dE", dE), ("dA", dA), ("hi", hi_f))):
                for j in range(SUB):
                    cols = slice(j, GE, SUB) if name in ("drel", "dE") else slice(j * P, (j + 1) * P)
                    last = T.transpose(ps[:, q, j * GP:j * GP + NG], mine[0:NG, cols], ident[0:NG, 0:NG])
                last.then_inc(idxT_mm, 1)
            pe.wait_ge(idxT_done, 6)

            def transpose_h0(b):
                pe.wait_ge(h0_ready, b + 1)
                if b >= 2:
                    pe.wait_ge(hT_done, b - 1)
                for f in range(FC):
                    last = T.transpose(ps[:, b % 2, f * P:(f + 1) * P], X[:, b, f * P:(f + 1) * P], ident[:])
                last.then_inc(hT_mm, 1)

            def first_half(b):
                pe.wait_ge(hT_done, b + 1)
                if b >= 2:
                    pe.wait_ge(u1_done, b - 1)
                for f in range(FC):
                    last = T.matmul(ps[:, 2 + b % 2, :], U[:, b, f * P:(f + 1) * P], WuT[:, f, :], start=f == 0, stop=f == FC - 1)
                last.then_inc(u1_mm, 1)

            for b in range(NT + 1):
                if b < NT:
                    transpose_h0(b)
                if b >= 1:
                    first_half(b - 1)
            pe.wait_ge(u1_mm, NT)
            T.sem_inc(group_done, SLOTS - 2)

            def group(s, n, turn):
                h = s % HOTS
                pe.wait_ge(add_step, (n + 1) * (SUB + 1))
                pe.wait_ge(hot_ready, n + 1)
                pe.wait_ge(ea_in[s], 16 * (turn + 1))
                for j in range(2):
                    T.matmul(ps[:, s, :], oneD[h][:, j, :].bitcast(F32), ea[s][:, j, :], start=j == 0, stop=False)
                pe.wait_ge(hotA_ready, n + 1)
                for j in range(SUB):
                    T.matmul(ps[:, 4 + s, j * KW:(j + 1) * KW], oneS[h][:, j, :], oneK[h][:, j, :], start=True, stop=True)
                pe.wait_ge(hi_ready, n + 1)
                for j in range(2):
                    T.matmul(ps[:, s, :], oneD[h][:, 2 + j, :], hi[h][:, j, :], start=False, stop=False)
                pe.wait_ge(lo_ready, n + 1)
                for j in range(2):
                    last = T.matmul(ps[:, s, :], oneD[h][:, 2 + j, :], lo[h][:, j, :], start=False, stop=j == 1)
                last.then_inc(group_done, 1)

            with pe.Fori(0, TURNS) as i:
                for s in range(SLOTS):
                    group(s, i * SLOTS + s, i)
            for s in range(3):
                group(s, TURNS * SLOTS + s, TURNS)

            pe.wait_ge(prep, PREP_ALL)
            uncovered = pe.value_load(nunc[0:1, 0:1], min_val=0, max_val=2 * E)
            with pe.If(uncovered > 0):
                pe.wait_ge(add_step, (NG + SLOTS) * (SUB + 1))
                T.sem_inc(gen_mm, 1)
                with pe.Fori(0, NT * NG) as n:
                    pe.wait_ge(gen_ea_in, 16 * n + 16)
                    pe.wait_ge(gen_hot, n + 1)
                    for j in range(SUB):
                        last = T.matmul(ps[:, 0, :], oneD[0][:, j, :].bitcast(F32), ea[0][:, j, :], start=j == 0, stop=j == SUB - 1)
                    last.then_inc(gen_mm, 1)
                with pe.Fori(0, NT * HB * NG) as n:
                    pe.wait_ge(gen_hot, n + NT * NG + 1)
                    for j in range(SUB):
                        last = T.matmul(ps[:, 0, 0:P], oneS[0][:, j, :], oneS[1][:, j, :], start=j == 0, stop=j == SUB - 1)
                    last.then_inc(gen_mm, 1)
                pe.nop()

            pe.wait_ge(summed, 1)
            pe.wait_ge(fold_step, 4)
            T.transpose(ps[0:1, 7, 0:P], most[:], ident[:]).then_inc(most_mm, 1)

            def windows():
                for n, w in enumerate(list(range(0, NW, 2)) + list(range(1, NW, 2))):
                    if n >= 2:
                        pe.wait_ge(win_add, n - 1)
                    for f in range(FC):
                        last = T.transpose(ps[:, 4 + n % 2, f * P:(f + 1) * P], SW[:, w, f * P:(f + 1) * P], ident[:])
                    last.then_inc(win_mm, 1)
                for b in range(NT):
                    last = T.matmul(ps[:, 6, b:b + 1], Dsum[:, b * P:(b + 1) * P], onesF[:, 0:1], start=True, stop=True)
                last.then_inc(deg_mm, 1)

            def times_A(exact, bank, c, q):
                for f in range(FC):
                    to, rows = ps[:, bank + f, 0:QC], slice(f * P, (f + 1) * P)
                    if exact:
                        T.matmul(to, Hh[:, c, rows].bitcast(F32), AF[:, c, bass.ds(q * QC, QC)], start=c == 0, stop=False)
                        last = T.matmul(to, Hl[:, c, rows].bitcast(F32), AF[:, c, bass.ds(q * QC, QC)], start=False, stop=c == NT - 1)
                    else:
                        T.matmul(to, Hh[:, c, rows], AR[:, c, bass.ds(q * QC, QC)], start=c == 0, stop=False)
                        last = T.matmul(to, Hl[:, c, rows], AR[:, c, bass.ds(q * QC, QC)], start=False, stop=c == NT - 1)
                return last

            def map_agg(b):
                if b >= 2:
                    pe.wait_ge(t_ready, b - 1)
                for f in range(FC):
                    last = T.matmul(ps[:, 4 + b % 2, :], aggT[:, f, b * P:(b + 1) * P], CT[:, f, :], start=f == 0, stop=f == FC - 1)
                last.then_inc(c_mm, 1)

            def layers(exact):
                pe.wait_ge(split0, NT)
                if exact:
                    pe.wait_ge(conv_exact, 1)
                for c in range(NT):
                    if not exact:
                        pe.wait_ge(conv, c + 1)
                    last = times_A(exact, 0, c, 0)
                last.then_inc(agg_mm, 1)
                windows()
                pe.wait_ge(win_add, NW)
                pe.wait_ge(deg_step, 2)
                for c in range(NT):
                    last = times_A(exact, 4, c, 1)
                last.then_inc(agg_mm, 1)
                for q in range(2, NQ):
                    pe.wait_ge(agg_done, q - 1)
                    for c in range(NT):
                        last = times_A(exact, (q % 2) * 4, c, q)
                    last.then_inc(agg_mm, 1)
                pe.wait_ge(agg_done, NQ)
                for b in range(NT + 6):
                    if b < NT:
                        map_agg(b)
                    if 4 <= b < NT + 4:
                        c = b - 4
                        pe.wait_ge(h1_ready, c + 1)
                        if c >= 2:
                            pe.wait_ge(h1T_done, c)
                        for f in range(FC):
                            last = T.transpose(ps[:, 6 + c % 2, f * P:(f + 1) * P], X[:, c, f * P:(f + 1) * P], ident[:])
                        last.then_inc(h1T_mm, 1)
                    if b >= 6:
                        pe.wait_ge(split1, b - 5)
                        last = times_A(exact, 0, b - 6, 0)
                last.then_inc(rst_mm, 1)
                pe.wait_ge(h1T_done, NT + 1)
                pe.wait_ge(t_ready, NT)
                for q in range(1, NQ):
                    if q >= 2:
                        pe.wait_ge(rst_done, q - 1)
                    for c in range(NT):
                        last = times_A(exact, (q % 2) * 4, c, q)
                    last.then_inc(rst_mm, 1)

            pe.wait_ge(most_ready, 2)
            large = pe.value_load(most1[0:1, 0:1], min_val=0, max_val=E + P)
            with pe.If(large > COUNT_MAX):
                layers(True)
            with pe.Else():
                layers(False)
            pe.wait_ge(w12_in, 32)
            pe.wait_ge(rst_done, NQ)
            T.sem_inc(hid_done, 4)
            with pe.Fori(0, NQ) as q:
                for k in range(KC):
                    pe.wait_ge(hid_done, q * KC + k + 1)
                    for f in range(FC):
                        last = T.matmul(ps[:, k % 4, 0:QC], W1s[:, f, k * P:(k + 1) * P], aggT[:, f, bass.ds(q * QC, QC)],
                                        start=f == 0, stop=f == FC - 1)
                    last.then_inc(hid_mm, 1)
            for b in range(NT):
                pe.wait_ge(hid_done, min(NQ, (b * P) // QC + 1) * KC + 4)
                if b >= 2:
                    pe.wait_ge(y_done, b - 1)
                for k in range(KC):
                    last = T.matmul(ps[:, 4 + b % 2, :], hid[:, k, b * P:(b + 1) * P], W2s[:, k, :], start=k == 0, stop=k == KC - 1)
                last.then_inc(y_mm, 1)


_INS = ['x', 'src', 'dst', 'edge_attr_512', 'L0_gnn_Wm', 'L0_gnn_bm', 'L0_gnn_Wu', 'L0_gnn_bu', 'L0_gnn_gamma',
        'L0_gnn_beta', 'L1_gnn_W1', 'L1_gnn_b1', 'L1_gnn_W2', 'L1_gnn_b2', 'L1_gnn_eps']
_OUTS = [((1250, 512), 'float32')]


def kernel(**inputs):
    import numpy as _np
    import concourse.bacc as _bacc
    from concourse import mybir as _mybir
    from concourse.bass_utils import run_bass_kernel_spmd as _run

    nc = _bacc.Bacc("TRN2", target_bir_lowering=False, num_devices=1)
    arrays, args = {}, []
    for name in _INS:
        a = _np.ascontiguousarray(inputs[name])
        arrays[f"in_{name}_dram"] = a
        args.append(nc.dram_tensor(f"in_{name}_dram", a.shape, _mybir.dt.from_np(a.dtype), kind="ExternalInput").ap())
    for i, (shape, dtype) in enumerate(_OUTS):
        dt = _mybir.dt.from_np(_np.dtype(dtype))
        args.append(nc.dram_tensor(f"out_{i}_dram", shape, dt, kind="ExternalOutput").ap())
    gnn_kernel(nc, *args)
    r = _run(nc, [arrays], core_ids=[0])
    return r.results[0]["out_0_dram"]
```

```python
from contextlib import ExitStack

import concourse.bass as bass
from concourse import mybir

F32 = mybir.dt.float32
F32R = mybir.dt.float32r
BF16 = mybir.dt.bfloat16
I32 = mybir.dt.int32
U16 = mybir.dt.uint16
ALU = mybir.AluOpType
ACT = mybir.ActivationFunctionType
AX = mybir.AxisListType

P = 128
SUB = 4
SLOTS = 4
ROUND = 8
HOTS = 2
W = 12
HALF = 64
EPS = 1e-5
COUNT_MAX = 4096
PREP_OFFS = 18
PREP_KEYS = 25
PREP_ALL = 27


def gnn_kernel(nc, x, src, dst, edge, Wm, bm, Wu, bu, gamma, beta, W1, b1, W2, b2, eps, out):
    N, D = x.shape
    E = edge.shape[0]
    HID = W1.shape[1]
    NT = -(-N // P)
    NP = NT * P
    TAIL = N - (NT - 1) * P
    FC = D // P
    KC = HID // P
    GE = SUB * P
    NG = -(-E // GE)
    ETAIL = E - (NG - 1) * GE
    GP = NG + 1
    HB = NT
    KW = HB * W
    NW = (NP - P) // HALF + 1
    AW = NP + W
    QS = [(0, 512), (512, 512), (1024, 256)]
    NQ = len(QS)
    TURNS = (NG - 1) // ROUND
    PEELED = TURNS * ROUND
    SPLIT = TURNS * 2 // 3
    assert ROUND % SLOTS == 0
    ORDER = list(range(4)) + list(range(8, NT)) + list(range(4, 8))
    EARLY = len(ORDER) - 4
    PAUSE = 2
    SLOT = [b if b < EARLY else b + PAUSE for b in range(NT)]
    H1_AT = [4, 5, 7, 9]
    WINDOWS = list(range(0, NW, 2)) + list(range(1, NW, 2))
    WU_ORDER = list(range(FC, 2 * FC)) + list(range(FC))
    assert ETAIL % SUB == 0 and D == GE and sum(n for _, n in QS) == NP and NG - PEELED >= HOTS and PEELED % SLOTS == 0
    assert len(QS) == 3 and QS[2][1] * 2 == 512

    at = [-(-nc.sbuf_base // 64) * 64]

    def place(name, shape, dt, offset=None):
        size = mybir.dt.size(dt)
        for n in shape[1:]:
            size *= n
        if offset is None:
            offset = at[0]
            at[0] += -(-size // 32) * 32
        return nc.alloc_sbuf_tensor_at(name, shape, dt, offset=offset), offset

    X, x_at = place("X", [P, NT, D], F32)
    Hl, _ = place("Hl", [P, NT, D], F32R, x_at)
    Hh, hh_at = place("Hh", [P, NT, D], F32R)
    NW1 = NT - FC
    Wu1T, _ = place("Wu1T", [P, FC, D], F32, hh_at + NW1 * D * 4)
    U, u_at = place("U", [P, NT, D], F32)
    A16, a16_at = place("A16", [P, HB, AW], U16)
    SW, sw_at = place("SW", [P, NW, D], F32)
    CT, _ = place("CT", [P, FC, D], F32)
    stream_at = at[0]

    def size_of(shape, dt):
        size = mybir.dt.size(dt)
        for n in shape[1:]:
            size *= n
        return size

    ea = [place(f"ea{s}", [P, SUB, D], F32)[0] for s in range(SLOTS)]
    hots_at = at[0]
    hi, lo, oneD, oneS, oneK = [], [], [], [], []
    for s in range(HOTS):
        for lst, name, shape, dt in ((hi, "hi", [P, 2, D], F32R), (lo, "lo", [P, 2, D], F32R), (oneD, "oneD", [P, SUB, P], F32R),
                                     (oneS, "oneS", [P, SUB, P], BF16), (oneK, "oneK", [P, SUB, KW], BF16)):
            lst.append(place(f"{name}{s}", shape, dt)[0])
    hots_size = (at[0] - hots_at) // HOTS
    hots1_at = hots_at + hots_size
    at[0] = max(at[0], stream_at + NT * NP * 4 + 3 * D * 4)
    WuN, _ = place("WuN", [P, FC, 2 * D], F32, stream_at)
    Wu2T, _ = place("Wu2T", [P, FC, D], F32, hh_at)
    WmN, _ = place("WmN", [P, FC, D], F32, u_at)
    bmB, _ = place("bmB", [P, FC, P], F32, u_at + 8192)
    AR, _ = place("AR", [P, NT, NP], F32R, stream_at)
    AF, _ = place("AF", [P, NT, NP], F32, stream_at)
    hid, _ = place("hid", [P, KC, NP], F32, stream_at)
    fold, _ = place("fold", [P, HB // 2, NP], U16, stream_at + 7 * NP * 4)
    spare = stream_at + NT * NP * 4
    gammaB, _ = place("gammaB", [P, D], F32, spare)
    betaB, _ = place("betaB", [P, D], F32, spare + 2048)
    b2B, _ = place("b2B", [P, D], F32, spare + 4096)
    aggT, _ = place("aggT", [P, FC, NP], F32, a16_at)
    W1s, _ = place("W1s", [P, FC, HID], F32, sw_at)
    W2s, _ = place("W2s", [P, KC, D], F32, sw_at + 16384)
    g_tmp = {}
    g_names = ["dst_f", "bigE", "bigA", "valid", "drel", "wrel", "dE", "dA", "hi_f", "lo_f", "key", "tmp"]
    g_places = [u_at + 10240 + n * GE * 4 for n in range(5)] + [hh_at + 8192 + n * GE * 4 for n in range(2)]
    g_places += [hots1_at + n * GE * 4 for n in range(5)]
    assert len(g_places) == len(g_names) and 5 * GE * 4 <= hots_size and u_at + 10240 + 5 * GE * 4 <= u_at + NT * D * 4
    for name, where in zip(g_names, g_places):
        g_tmp[name], _ = place("g_" + name, [P, GE], F32, where)
    dst_f, bigE, bigA, valid, drel, wrel, dE, dA, hi_f, lo_f, key, tmpf = g_tmp.values()
    dst_i, _ = place("dst_i", [P, GE], I32, sw_at)
    src_i, _ = place("src_i", [P, GE], I32, sw_at + 2048)
    NI = 4
    hi_i, _ = place("hi_i", [P, GE], I32, sw_at + 4096)
    lo_i, _ = place("lo_i", [P, GE], I32, sw_at + 6144)
    idx_at = -(-at[0] // 32) * 32
    idxT = {n: place("T_" + n, [P, SUB, GP], F32)[0] for n in ("drel", "key", "lo", "dE", "dA", "hi")}
    iotaF, _ = place("iotaF", [P, P], F32)
    iotaB, _ = place("iotaB", [P, P], BF16)
    ident, _ = place("ident", [P, P], F32)
    pid, _ = place("pid", [P, 1], F32)
    onesF, _ = place("onesF", [P, 1], F32)
    mhalf, _ = place("mhalf", [P, NT], F32)
    buB, buB_at = place("buB", [P, D], F32)
    cbB, _ = place("cbB", [P, D], F32)
    bmC, _ = place("bmC", [P, FC], F32)
    b1C, _ = place("b1C", [P, KC], F32)
    epsC, _ = place("epsC", [P, 1], F32)
    eps1, _ = place("eps1", [P, 1], F32)
    m4, _ = place("m4", [P, 8], F32)
    wf, _ = place("wf", [P, 4], F32)
    wi, _ = place("wi", [P, 2], I32)
    offs, _ = place("offs", [P, 8], U16)
    offrow, _ = place("offrow", [1, NG * 8], U16)
    square = [place(f"square{h}", [P, SUB, P], BF16)[0] for h in range(HOTS)]
    most, _ = place("most", [P, 1], F32)
    most1_f, _ = place("most1_f", [1, 1], F32)
    most1, _ = place("most1", [1, 1], I32)
    nunc_f, _ = place("nunc_f", [1, 2], F32)
    nunc, _ = place("nunc", [1, 2], I32)
    stats, _ = place("stats", [P, NT, 6], F32)
    mv, _ = place("mv", [P, NT, 2], F32)
    stats2, _ = place("stats2", [P, NT, 6], F32, buB_at)
    mv2, _ = place("mv2", [P, NT, 2], F32)
    ve, _ = place("ve", [P, NT], F32)
    ve2, _ = place("ve2", [P, NT], F32)
    rs, _ = place("rs", [P, NT], F32)
    rs2, _ = place("rs2", [P, NT], F32)
    nb, _ = place("nb", [P, NT], F32)
    degs, _ = place("degs", [P, NT], F32)
    rdeg, _ = place("rdeg", [P, NT], F32)
    has, _ = place("has", [P, NT], F32)
    TB = 3
    Dsum, _ = place("Dsum", [P, NP], F32, idx_at)
    tt = [place(f"tt{i}", [P, D], F32, idx_at + i * 2048)[0] for i in range(TB)]
    h0t = [place(f"h0t{i}", [P, D], F32, sw_at + 32768 + i * 2048)[0] for i in range(TB)]
    xt = [place(f"xt{i}", [P, D], F32, a16_at + 20480 + i * 2048)[0] for i in range(2)] + [place("xt2", [P, D], F32)[0]]
    assert at[0] <= nc.sbuf_usable_end, at[0] - nc.sbuf_usable_end

    ctx = ExitStack()
    with ctx:
        ps = ctx.enter_context(nc.psum_tensor("ps", [P, 8, 512], F32))

        def sem(name):
            return ctx.enter_context(nc.semaphore(name))

        pads_set = sem("pads_set")
        consts = sem("consts")
        idx_in = sem("idx_in")
        x_in = sem("x_in")
        wu1_in = sem("wu1_in")
        wu2_in = sem("wu2_in")
        wm_in = sem("wm_in")
        small_in = sem("small_in")
        prep = sem("prep")
        ident_ready = sem("ident_ready")
        offs_in = sem("offs_in")
        a_zero = sem("a_zero")
        idxT_mm = sem("idxT_mm")
        idxT_done = sem("idxT_done")
        idxT_out = sem("idxT_out")
        outside_ready = sem("outside_ready")
        wuT_mm = sem("wuT_mm")
        wuT_done = sem("wuT_done")
        ln0 = sem("ln0")
        ve_ready = sem("ve_ready")
        rs_ready = sem("rs_ready")
        nb_ready = sem("nb_ready")
        h0_ready = sem("h0_ready")
        hT_mm = sem("hT_mm")
        hT_done = sem("hT_done")
        u1_mm = sem("u1_mm")
        u1_done = sem("u1_done")
        bmB_done = sem("bmB_done")
        ct_mm = sem("ct_mm")
        ct_done = sem("ct_done")
        group_done = sem("group_done")
        ea_in = [sem(f"ea_in{s}") for s in range(SLOTS)]
        hi_ready = sem("hi_ready")
        lo_ready = sem("lo_ready")
        hi0_ready = sem("hi0_ready")
        low0_ready = [sem("low0_pool"), sem("low0_dve")]
        square_ready = sem("square_ready")
        hotA_ready = sem("hotA_ready")
        h0t_ready = sem("h0t_ready")
        hi1_ready = sem("hi1_ready")
        split1 = sem("split1")
        hotD_ready = sem("hotD_ready")
        hotK_ready = sem("hotK_ready")
        add_step = sem("add_step")
        sum_step = sem("sum_step")
        gen_ea_in = sem("gen_ea_in")
        gen_hot = sem("gen_hot")
        gen_mm = sem("gen_mm")
        gen_add = sem("gen_add")
        gen_step = sem("gen_step")
        summed = sem("summed")
        fold_step = sem("fold_step")
        most_mm = sem("most_mm")
        most_ready = sem("most_ready")
        conv = sem("conv")
        conv_exact = sem("conv_exact")
        dsum_ready = sem("dsum_ready")
        deg_mm = sem("deg_mm")
        deg_step = sem("deg_step")
        agg_mm = sem("agg_mm")
        agg_done = sem("agg_done")
        c_mm = sem("c_mm")
        t_ready = sem("t_ready")
        g_ready = sem("g_ready")
        o_sum = sem("o_sum")
        o_stats = sem("o_stats")
        o_aggr = sem("o_aggr")
        centered = sem("centered")
        x1_stats = sem("x1_stats")
        x1_aggr = sem("x1_aggr")
        ve1_ready = sem("ve1_ready")
        rs1_ready = sem("rs1_ready")
        ve2_ready = sem("ve2_ready")
        rs2_ready = sem("rs2_ready")
        x1_ready = sem("x1_ready")
        nb2_ready = sem("nb2_ready")
        h1_ready = sem("h1_ready")
        late_in = sem("late_in")
        w12_in = sem("w12_in")
        xt_in = [sem(f"xt_in{i}") for i in range(TB)]
        xb_ready = sem("xb_ready")
        eps_ready = sem("eps_ready")
        win_mm = sem("win_mm")
        win_done = sem("win_done")
        ab_mm = sem("ab_mm")
        h1T_mm = sem("h1T_mm")
        h1T_done = sem("h1T_done")
        rst_mm = sem("rst_mm")
        rst_done = sem("rst_done")
        hid_mm = sem("hid_mm")
        hid_done = sem("hid_done")
        res_step = sem("res_step")
        y_mm = sem("y_mm")
        y_done = sem("y_done")
        stored = sem("stored")

        block = ctx.enter_context(nc.Block())

        edge_g = edge[0:(NG - 1) * GE, :].rearrange("(g p j) d -> g p j d", p=P, j=SUB)
        edge_tail = edge[(NG - 1) * GE:E, :].rearrange("(p j) d -> p j d", j=SUB)
        TP = ETAIL // SUB

        @block.sync
        def _(sp):
            sp.wait_ge(pads_set, 2)
            for t, a in ((dst_i, dst), (src_i, src)):
                sp.dma_start(t[0:NG - 1, :], a[0:(NG - 1) * GE].rearrange("(g e) -> g e", e=GE)).then_inc(idx_in, 16)
                sp.dma_start(t[NG - 1:NG, 0:ETAIL], a[(NG - 1) * GE:E].rearrange("(g e) -> g e", g=1)).then_inc(idx_in, 16)
            sp.dma_start(WuN[:, :, 0:D], Wu[:, 0:D].rearrange("(o p) i -> p o i", p=P)).then_inc(wu1_in, 16)
            sp.dma_start(WmN[:], Wm.rearrange("(m p) i -> p m i", p=P)).then_inc(wm_in, 16)
            sp.wait_ge(pads_set, 3)
            sp.dma_start(X[:, 0:NT - 1, :], x[0:(NT - 1) * P, :].rearrange("(b p) d -> p b d", p=P)).then_inc(x_in, 16)
            sp.dma_start(X[0:TAIL, NT - 1, :], x[(NT - 1) * P:N, :]).then_inc(x_in, 16)
            sp.dma_start(buB[:], bu.rearrange("(a d) -> a d", a=1).broadcast_to([P, D])).then_inc(small_in, 16)
            sp.dma_start(bmC[:], bm.rearrange("(m p) -> p m", p=P), allow_slow_non_contiguous=True).then_inc(small_in, 16)
            sp.dma_start(b1C[:], b1.rearrange("(k p) -> p k", p=P), allow_slow_non_contiguous=True).then_inc(small_in, 16)
            sp.dma_start(epsC[:], eps.rearrange("(a d) -> a d", a=1).broadcast_to([P, 1])).then_inc(small_in, 16)
            sp.wait_ge(prep, PREP_OFFS)
            sp.dma_start(offrow[0:1, :], offs[0:NG, :]).then_inc(offs_in, 16)

            def load_group(s, n):
                sp.wait_ge(group_done, n + 1)
                sp.dma_start(ea[s][:], edge_g[bass.ds(n, 1)].rearrange("g p j d -> (g p) j d")).then_inc(ea_in[s], 16)

            with sp.Fori(0, TURNS) as i:
                for r in range(ROUND):
                    load_group(r % SLOTS, i * ROUND + r)
            for n in range(PEELED, NG - 1):
                load_group(n % SLOTS, n)
            sp.wait_ge(group_done, NG)
            sp.dma_start(ea[(NG - 1) % SLOTS][0:TP, :, :], edge_tail).then_inc(ea_in[(NG - 1) % SLOTS], 16)

            sp.wait_ge(group_done, NG + SLOTS)
            sp.wait_ge(prep, PREP_ALL)
            uncovered = sp.value_load(nunc[0:1, 0:1], min_val=0, max_val=2 * E)
            with sp.If(uncovered > 0):
                with sp.Fori(0, NT) as b:
                    with sp.Fori(0, NG - 1) as g:
                        sp.wait_ge(gen_mm, b * NG + g + 1)
                        sp.dma_start(ea[0][:], edge_g[bass.ds(g, 1)].rearrange("g p j d -> (g p) j d")).then_inc(gen_ea_in, 16)
                    sp.wait_ge(gen_mm, b * NG + NG)
                    sp.dma_start(ea[0][0:TP, :, :], edge_tail).then_inc(gen_ea_in, 16)
                sp.nop()

            sp.wait_ge(summed, 1)
            for t, a in ((gammaB, gamma), (betaB, beta), (b2B, b2)):
                sp.dma_start(t[:], a.rearrange("(a d) -> a d", a=1).broadcast_to([P, D])).then_inc(late_in, 16)

            def load_x(b):
                if b >= TB:
                    sp.wait_ge(x1_ready, b - TB + 1)
                elif b == 0:
                    sp.wait_ge(conv, NT)
                    sp.wait_ge(fold_step, 1)
                    sp.wait_ge(conv_exact, 1)
                t = ORDER[b]
                rows = P if t < NT - 1 else TAIL
                sp.dma_start(xt[b % TB][0:rows, :], x[t * P:t * P + rows, :]).then_inc(xt_in[b % TB], 16)

            for b in range(TB):
                load_x(b)
            sp.wait_ge(win_mm, NW)
            sp.dma_start(W1s[:], W1.rearrange("(f p) h -> p f h", p=P)).then_inc(w12_in, 16)
            sp.dma_start(W2s[:], W2.rearrange("(k p) d -> p k d", p=P)).then_inc(w12_in, 16)
            for b in range(TB, NT):
                load_x(b)
            for b in range(NT):
                rows = P if b < NT - 1 else TAIL
                sp.wait_ge(y_done, b + 1)
                sp.dma_start(out[b * P:b * P + rows, :], U[0:rows, b, :]).then_inc(stored, 16)
            sp.wait_ge(stored, 16 * NT)

        @block.gpsimd
        def _(pool):
            nc.gpsimd.memset(dst_i[:], NP - 1).then_inc(pads_set, 1)
            nc.gpsimd.memset(src_i[:], 0).then_inc(pads_set, 1)
            nc.gpsimd.memset(X[:, NT - 1, :], 0.0).then_inc(pads_set, 1)
            nc.gpsimd.iota(iotaF[:], [[1, P]], base=0, channel_multiplier=0, allow_small_or_imprecise_dtypes=True).then_inc(consts, 1)
            nc.gpsimd.iota(pid[:], [[1, 1]], base=0, channel_multiplier=1, allow_small_or_imprecise_dtypes=True).then_inc(consts, 1)
            nc.gpsimd.iota(iotaB[:], [[1, P]], base=0, channel_multiplier=0, allow_small_or_imprecise_dtypes=True).then_inc(consts, 1)
            nc.gpsimd.memset(mhalf[:], -0.5).then_inc(consts, 1)
            nc.gpsimd.memset(onesF[:], 1.0).then_inc(consts, 1)
            nc.gpsimd.memset(offs[:], 0).then_inc(consts, 1)
            nc.gpsimd.memset(A16[:].bitcast(I32), 0).then_inc(a_zero, 1)
            nc.gpsimd.memset(SW[:, NI:, :], 0.0).then_inc(a_zero, 1)
            G = slice(0, NG)
            pool.wait_ge(prep, PREP_OFFS)
            nc.gpsimd.tensor_scalar(valid[G, :], dst_f[G, :], 1.0, None, ALU.add).then_inc(outside_ready, 1)
            pool.wait_ge(outside_ready, 1)
            nc.gpsimd.tensor_tensor(bigE[G, :], valid[G, :], bigE[G, :], ALU.mult).then_inc(outside_ready, 1)
            nc.gpsimd.tensor_tensor(bigA[G, :], valid[G, :], bigA[G, :], ALU.mult).then_inc(outside_ready, 1)
            pool.wait_ge(outside_ready, 3)
            nc.gpsimd.tensor_scalar(dE[G, :], bigE[G, :], 1.0, None, ALU.subtract).then_inc(outside_ready, 1)
            nc.gpsimd.tensor_scalar(dA[G, :], bigA[G, :], 1.0, None, ALU.subtract).then_inc(outside_ready, 1)
            pool.wait_ge(prep, PREP_KEYS)
            nc.gpsimd.memset(SW[:, 0:NI, :], 0.0).then_inc(a_zero, 1)

            def low_parts(s, n, turn):
                h = s % HOTS
                pool.wait_ge(group_done, n + SLOTS - HOTS + 1)
                pool.wait_ge(ea_in[s], 16 * (turn + 1))
                pool.wait_ge(hi_ready, n + 1)
                nc.gpsimd.tensor_tensor(lo[h][:], ea[s][:, 2:4, :], hi[h][:].bitcast(F32), ALU.subtract).then_inc(lo_ready, 1)

            for first, end in ((0, SPLIT), (SPLIT, TURNS)):
                with pool.Fori(first, end) as i:
                    for r in range(ROUND):
                        low_parts(r % SLOTS, i * ROUND + r, i * (ROUND // SLOTS) + r // SLOTS)
                if first == 0:
                    pool.wait_ge(consts, 6)
                    pool.wait_ge(ve_ready, 1)
                    nc.gpsimd.tensor_tensor(rs[:], ve[:], mhalf[:], ALU.pow).then_inc(rs_ready, 1)
            for n in range(PEELED, NG):
                low_parts(n % SLOTS, n, n // SLOTS)

            with pool.Fori(0, NW1) as b:
                pool.wait_ge(hi0_ready, b + 1)
                pool.wait_ge(hT_mm, b + 1)
                nc.gpsimd.tensor_tensor(Hl[:, bass.ds(b, 1), :], X[:, bass.ds(b, 1), :], Hh[:, bass.ds(b, 1), :].bitcast(F32),
                                        ALU.subtract).then_inc(low0_ready[0], 1)

            pool.wait_ge(win_mm, NW)
            pool.wait_ge(low0_ready[1], 1)

            def ahead(b):
                pool.wait_ge(xt_in[b % TB], 16 * (b // TB + 1))
                nc.gpsimd.tensor_tensor(xt[b % TB][:], xt[b % TB][:], betaB[:], ALU.add).then_inc(xb_ready, 1)
                nc.gpsimd.tensor_tensor(h0t[b % TB][:], Hh[:, ORDER[b], :].bitcast(F32), Hl[:, ORDER[b], :].bitcast(F32), ALU.add).then_inc(h0t_ready, 1)

            pool.wait_ge(late_in, 48)
            for b in range(TB):
                ahead(b)
            for k in range(SLOT[-1] + 2):
                if k in SLOT:
                    b = SLOT.index(k)
                    pool.wait_ge(ve1_ready, b + 1)
                    nc.gpsimd.tensor_tensor(rs[:, b:b + 1], ve[:, b:b + 1], mhalf[:, 0:1], ALU.pow).then_inc(rs1_ready, 1)
                if k - 1 in SLOT:
                    b = SLOT.index(k - 1)
                    pool.wait_ge(ve2_ready, b + 1)
                    nc.gpsimd.tensor_tensor(rs2[:, b:b + 1], ve2[:, b:b + 1], mhalf[:, 0:1], ALU.pow).then_inc(rs2_ready, 1)
                    if b + TB < NT:
                        ahead(b + TB)
            pool.wait_ge(h1_ready, NT)
            pool.wait_ge(split1, NT)
            with pool.Fori(0, NT) as b:
                t = U[:, bass.ds(b, 1), :]
                nc.gpsimd.tensor_tensor(t, t, b2B[:].rearrange("p (a d) -> p a d", a=1), ALU.add).then_inc(res_step, 1)
                pool.wait_ge(res_step, b * 3 + 1)
                nc.gpsimd.tensor_tensor(t, t, Hh[:, bass.ds(b, 1), :].bitcast(F32), ALU.add).then_inc(res_step, 1)
                pool.wait_ge(res_step, b * 3 + 2)
                nc.gpsimd.tensor_tensor(t, t, Hl[:, bass.ds(b, 1), :].bitcast(F32), ALU.add).then_inc(res_step, 1)

        @block.scalar
        def _(act):
            act.dma_start(WuN[:, :, D:], Wu[:, D:].rearrange("(o p) i -> p o i", p=P)).then_inc(wu2_in, 16)

            def wuT(n):
                k = WU_ORDER[n]
                act.wait_ge(wuT_mm, n + 1)
                nc.scalar.copy(Wu1T[:, k, :] if k < FC else Wu2T[:, k - FC, :], ps[:, 6 + n % 2, :]).then_inc(wuT_done, 1)

            def ct(k):
                act.wait_ge(ct_mm, k + 1)
                nc.scalar.copy(CT[:, k, :], ps[:, 6 + k % 2, :]).then_inc(ct_done, 1)

            for n in range(2 * FC):
                wuT(n)
            for k in range(3):
                ct(k)
            for q, name in ((3, "hi"), (4, "dE"), (5, "dA")):
                act.wait_ge(idxT_mm, q + 1)
                nc.scalar.copy(idxT[name][:, :, 0:NG], ps[:, q, 0:SUB * GP].rearrange("p (j g) -> p j g", j=SUB)[:, :, 0:NG]).then_inc(idxT_out, 1)

            def high_parts(s, n, turn):
                h = s % HOTS
                act.wait_ge(group_done, n + SLOTS - HOTS + 1)
                for j in range(SUB):
                    ins = nc.scalar.activation(square[h][:, j, :], iotaF[:], ACT.Square, bias=idxT["lo"][:, j, bass.ds(n, 1)], scale=-1.0)
                ins.then_inc(square_ready, 1)
                act.wait_ge(ea_in[s], 16 * (turn + 1))
                nc.scalar.copy(hi[h][:], ea[s][:, 2:4, :]).then_inc(hi_ready, 1)
                act.wait_ge(square_ready, n + 1)
                nc.scalar.activation(oneS[h][:], square[h][:], ACT.Relu, bias=onesF[:, 0:1], scale=-1.0).then_inc(hotA_ready, 1)

            act.wait_ge(idxT_done, 3)
            with act.Fori(0, TURNS) as i:
                for r in range(ROUND):
                    high_parts(r % SLOTS, i * ROUND + r, i * (ROUND // SLOTS) + r // SLOTS)
            for n in range(PEELED, NG):
                high_parts(n % SLOTS, n, n // SLOTS)

            def transposed_h0(b):
                act.wait_ge(hT_mm, b + 1)
                nc.scalar.copy(U[:, b, :], ps[:, 3 + 4 * (b % 2), :]).then_inc(hT_done, 1)

            def h0(b):
                nc.scalar.activation(X[:, b, :], X[:, b, :], ACT.Relu, bias=nb[:, b:b + 1], scale=rs[:, b:b + 1]).then_inc(h0_ready, 1)

            act.wait_ge(nb_ready, 1)
            h0(0)
            h0(1)
            transposed_h0(0)
            transposed_h0(1)
            h0(2)
            h0(3)
            act.wait_ge(summed, 1)
            for b in range(NT):
                if b + 4 < NT:
                    h0(b + 4)
                if b < NW1:
                    act.wait_ge(h0_ready, b + 1)
                    nc.scalar.copy(Hh[:, b, :], X[:, b, :]).then_inc(hi0_ready, 1)
                if b == 7:
                    act.wait_ge(dsum_ready, 1)
                nc.scalar.copy(AR[:, b, :], A16[:, b, 0:NP]).then_inc(conv, 1)
                if b + 2 < NT:
                    transposed_h0(b + 2)
            act.wait_ge(most_ready, 2)
            large = act.value_load(most1[0:1, 0:1], min_val=0, max_val=E + P)
            act.wait_ge(conv, NT)
            with act.If(large > COUNT_MAX):
                for c in range(NT):
                    ins = nc.scalar.copy(AF[:, c, :], A16[:, c, 0:NP])
                ins.then_inc(conv_exact, 1)
            with act.Else():
                nc.scalar.sem_inc(conv_exact, 1)
            act.wait_ge(u1_mm, NT)
            act.wait_ge(h0_ready, NT)
            for b in range(NW1, NT):
                nc.scalar.copy(Hh[:, b, :], X[:, b, :]).then_inc(hi0_ready, 1)
            act.wait_ge(small_in, 64)
            nc.scalar.activation(eps1[:], epsC[:], ACT.Copy, bias=1.0).then_inc(eps_ready, 1)
            act.wait_ge(fold_step, 1)
            act.wait_ge(conv_exact, 1)
            for n, w in enumerate(WINDOWS[0:(NW + 1) // 2]):
                act.wait_ge(win_mm, n + 1)
                nc.scalar.copy(aggT[:, :, w * HALF:w * HALF + P], ps[:, 6 + n % 2, :].rearrange("p (f n) -> p f n", f=FC)).then_inc(win_done, 1)

            def gelu(b):
                act.wait_ge(t_ready, b + 1)
                nc.scalar.activation(tt[b % TB][:], tt[b % TB][:], ACT.Gelu).then_inc(g_ready, 1)

            def h1(b):
                t = ORDER[b]
                act.wait_ge(nb2_ready, b + 1)
                act.wait_ge(h0t_ready, b + 1)
                act.wait_ge(ab_mm, b + 1)
                nc.scalar.activation(X[:, t, :], U[:, t, :], ACT.Relu, bias=nb[:, b:b + 1], scale=rs2[:, b:b + 1]).then_inc(h1_ready, 1)

            def h1_high(b):
                act.wait_ge(h1_ready, b + 1)
                nc.scalar.copy(Hh[:, ORDER[b], :], X[:, ORDER[b], :]).then_inc(hi1_ready, 1)

            def h1T(b):
                t = ORDER[b]
                act.wait_ge(h1T_mm, b + 1)
                act.wait_ge(c_mm, b + 1)
                nc.scalar.activation(aggT[:, :, t * P:(t + 1) * P], ps[:, 6 + b % 2, :].rearrange("p (f n) -> p f n", f=FC),
                                     ACT.Copy, scale=eps1[:, 0:1]).then_inc(h1T_done, 1)

            act.wait_ge(eps_ready, 1)
            for k in range(SLOT[-1] + 5):
                for work, lag in ((gelu, 0), (h1, 3), (h1_high, 3), (h1T, 3)):
                    if k - lag in SLOT:
                        work(SLOT.index(k - lag))
            act.wait_ge(rst_mm, 4)

            def hidden(start, cols, n):
                for k in range(KC):
                    act.wait_ge(hid_mm, n * KC + k + 1)
                    nc.scalar.activation(hid[:, k, bass.ds(start, cols)], ps[:, k % 4, 0:cols], ACT.Relu,
                                         bias=b1C[:, k:k + 1]).then_inc(hid_done, 1)

            with act.Fori(0, NQ - 1) as q:
                hidden(q * 512, 512, q)
            hidden(QS[-1][0], N - QS[-1][0], NQ - 1)

        @block.vector
        def _(dve):
            V = nc.vector
            count = [0]

            def step(ins):
                count[0] += 1
                ins.then_inc(prep, 1)
                dve.wait_ge(prep, count[0])

            dve.wait_ge(consts, 6)
            V.tensor_scalar(ident[:], iotaF[:], pid[:, 0:1], None, ALU.is_equal).then_inc(ident_ready, 1)
            dve.wait_ge(idx_in, 64)
            G = slice(0, NG)

            def tiles(t):
                return t[G, :].rearrange("g (j p) -> g j p", j=SUB)

            step(V.tensor_copy(dst_f[G, :], dst_i[G, :]))
            step(V.tensor_reduce(m4[G, 0:SUB], tiles(dst_f), AX.X, ALU.min))
            step(V.tensor_reduce(m4[G, 4:5], m4[G, 0:SUB], AX.X, ALU.min))
            step(V.tensor_copy(offs[G, 0:SUB], m4[G, 0:SUB]))
            step(V.tensor_copy(wi[G, 0:1], m4[G, 4:5]))
            step(V.tensor_scalar(wi[G, 1:2], wi[G, 0:1], 6, None, ALU.logical_shift_right))
            step(V.tensor_copy(wf[G, 0:1], wi[G, 1:2]))
            step(V.tensor_scalar(wf[G, 1:2], wf[G, 0:1], float(NW - 1), None, ALU.min))
            step(V.tensor_copy(offs[G, 4:5], wf[G, 1:2]))
            step(V.tensor_scalar(wf[G, 2:3], wf[G, 1:2], float(HALF), None, ALU.mult))
            step(V.tensor_scalar(drel[G, :], dst_f[G, :], wf[G, 2:3], None, ALU.subtract))
            step(V.tensor_tensor(tiles(wrel), tiles(dst_f), m4[G, 0:SUB].rearrange("g (j a) -> g j a", a=1).broadcast_to([NG, SUB, P]), ALU.subtract))
            step(V.tensor_scalar(valid[G, :], dst_f[G, :], float(N), None, ALU.is_lt))
            step(V.scalar_tensor_tensor(bigE[G, :], drel[G, :], float(P), valid[G, :], ALU.is_ge, ALU.mult))
            step(V.scalar_tensor_tensor(bigA[G, :], wrel[G, :], float(W), valid[G, :], ALU.is_ge, ALU.mult))
            step(V.scalar_tensor_tensor(tmpf[G, :], bigE[G, :], 1.0, bigA[G, :], ALU.mult, ALU.add))
            step(V.tensor_reduce(m4[G, 5:6], tmpf[G, :], AX.X, ALU.add))
            step(V.tensor_copy(offs[G, 5:6], m4[G, 5:6]))
            assert count[0] == PREP_OFFS
            step(V.tensor_scalar(hi_i[G, :], src_i[G, :], 7, None, ALU.logical_shift_right))
            step(V.tensor_scalar(lo_i[G, :], src_i[G, :], P - 1, None, ALU.bitwise_and))
            step(V.tensor_copy(hi_f[G, :], hi_i[G, :]))
            step(V.tensor_copy(lo_f[G, :], lo_i[G, :]))
            step(V.scalar_tensor_tensor(key[G, :], hi_f[G, :], float(W), wrel[G, :], ALU.mult, ALU.add))
            step(V.tensor_scalar(tmpf[G, :], wrel[G, :], float(W), 4096.0, ALU.is_ge, ALU.mult))
            step(V.tensor_tensor(key[G, :], key[G, :], tmpf[G, :], ALU.add))
            assert count[0] == PREP_KEYS
            dve.wait_ge(small_in, 64)
            V.tensor_copy(bmB[:], bmC[:].rearrange("p (m a) -> p m a", a=1).broadcast_to([P, FC, P])).then_inc(bmB_done, 1)

            dve.wait_ge(x_in, 32)
            for b in range(4):
                V.bn_stats(stats[:, b, :], X[:, b, :]).then_inc(ln0, 1)
            for q, name in enumerate(("drel", "key", "lo")):
                dve.wait_ge(idxT_mm, q + 1)
                V.tensor_copy(idxT[name][:, :, 0:NG], ps[:, q, 0:SUB * GP].rearrange("p (j g) -> p j g", j=SUB)[:, :, 0:NG]).then_inc(idxT_done, 1)
            dve.wait_ge(offs_in, 16)
            step(V.tensor_reduce(nunc_f[0:1, 0:1], offrow[0:1, :].rearrange("a (g k) -> a k g", k=8)[:, 5, :], AX.X, ALU.add))
            step(V.tensor_copy(nunc[0:1, 0:1], nunc_f[0:1, 0:1]))
            assert count[0] == PREP_ALL

            def one_hots_dst(s, n, half):
                js = slice(2 * half, 2 * half + 2)
                n1 = idxT["drel"][:, js, bass.ds(n, 1)].broadcast_to([P, 2, P])
                V.tensor_tensor(oneD[s % HOTS][:, js, :], iotaF[:].rearrange("p (a n) -> p a n", a=1).broadcast_to([P, 2, P]), n1,
                                ALU.is_equal).then_inc(hotD_ready, 1)

            def one_hots_key(s, n):
                n1 = idxT["key"][:, :, bass.ds(n, 1)].broadcast_to([P, SUB, KW])
                V.tensor_tensor(oneK[s % HOTS][:], iotaF[:, 0:KW].rearrange("p (a n) -> p a n", a=1).broadcast_to([P, SUB, KW]), n1,
                                ALU.is_equal).then_inc(hotK_ready, 1)

            def offsets(n):
                _, loaded = nc.values_load_multi_w_load_instructions(
                    offrow[0:1, bass.ds(n * 8, SUB + 1)], engines=(mybir.EngineType.DVE,), min_val=0, max_val=NP - 1,
                    skip_runtime_bounds_check_because="each is the least of indices of nodes, or a window")
                window = nc.s_assert_within(loaded[SUB], 0, NW - 1, skip_runtime_bounds_check_because="it was clamped to the last window")
                return loaded[0:SUB], window

            def add_up(s, n, at_cols, ahead, more=None):
                first, window = at_cols
                dve.wait_ge(group_done, n + SLOTS + 1)

                def add_counts(j):
                    cols = A16[:, :, bass.ds(first[j], W)]
                    dve.wait_ge(add_step, (n + SLOTS) * SUB + j)
                    V.tensor_tensor(cols, ps[:, 4 + s, j * KW:(j + 1) * KW].rearrange("p (h w) -> p h w", w=W), cols, ALU.add).then_inc(add_step, 1)

                if ahead:
                    one_hots_dst(s, n + HOTS, 0)
                add_counts(0)
                if ahead:
                    one_hots_dst(s, n + HOTS, 1)
                add_counts(1)
                if ahead:
                    one_hots_key(s, n + HOTS)
                add_counts(2)
                dve.wait_ge(sum_step, n + SLOTS)
                t = SW[:, bass.ds(window, 1), :]
                V.tensor_tensor(t, ps[:, s, :].rearrange("p (a d) -> p a d", a=1), t, ALU.add).then_inc(sum_step, 1)
                following = offsets(n + 1) if more else None
                add_counts(3)
                return following

            for n in range(HOTS):
                if n == 1:
                    dve.wait_ge(idxT_mm, 6)
                one_hots_dst(n, n, 0)
                one_hots_dst(n, n, 1)
                one_hots_key(n, n)
            dve.wait_ge(a_zero, 3)
            V.sem_inc(add_step, SLOTS * SUB)
            V.sem_inc(sum_step, SLOTS)
            for b in range(4, NT):
                V.bn_stats(stats[:, b, :], X[:, b, :]).then_inc(ln0, 1)
            dve.wait_ge(ln0, NT)
            for b in range(NT):
                V.bn_aggr(mv[:, b, :], stats[:, b, :]).then_inc(ln0, 1)
            dve.wait_ge(ln0, 2 * NT)
            V.tensor_scalar(ve[:], mv[:, :, 1], EPS, None, ALU.add).then_inc(ve_ready, 1)

            def product_out(n):
                dve.wait_ge(ct_mm, n + 1)
                V.tensor_copy(CT[:, n, :] if n < FC else cbB[:], ps[:, 6 + n % 2, :]).then_inc(ct_done, 1)

            product_out(FC - 1)
            for first, end in ((0, SPLIT), (SPLIT, TURNS)):
                with dve.Fori(first, end) as i:
                    where = offsets(i * ROUND)
                    for r in range(ROUND):
                        where = add_up(r % SLOTS, i * ROUND + r, where, True, r < ROUND - 1)
                if first == 0:
                    product_out(FC)
                    dve.wait_ge(rs_ready, 1)
                    V.scalar_tensor_tensor(nb[:], mv[:, :, 0], -1.0, rs[:], ALU.mult, ALU.mult).then_inc(nb_ready, 1)
            where = offsets(PEELED)
            for n in range(PEELED, NG):
                where = add_up(n % SLOTS, n, where, n + HOTS < NG, n < NG - 1)
            dve.wait_ge(add_step, (NG + SLOTS) * SUB)
            dve.wait_ge(sum_step, NG + SLOTS)

            uncovered = dve.value_load(nunc[0:1, 0:1], min_val=0, max_val=2 * E)
            with dve.If(uncovered > 0):
                with dve.Fori(0, NT) as b:
                    with dve.Fori(0, NG) as g:
                        dve.wait_ge(gen_mm, b * NG + g + 1)
                        for j in range(SUB):
                            last = V.tensor_scalar(oneD[0][:, j, :], iotaF[:], idxT["dE"][:, j, bass.ds(g, 1)], None, ALU.is_equal)
                        last.then_inc(gen_hot, 1)
                        dve.wait_ge(gen_mm, b * NG + g + 2)
                        V.tensor_tensor(SW[:, bass.ds(b * (P // HALF), 1), :], ps[:, 0, :].rearrange("p (a d) -> p a d", a=1),
                                        SW[:, bass.ds(b * (P // HALF), 1), :], ALU.add).then_inc(gen_add, 1)
                        dve.wait_ge(gen_add, b * NG + g + 1)
                    V.tensor_scalar(idxT["dE"][:, :, 0:NG], idxT["dE"][:, :, 0:NG], float(-P), None, ALU.add).then_inc(gen_step, 1)
                    dve.wait_ge(gen_step, b + 1)
                with dve.Fori(0, NT) as b:
                    with dve.Fori(0, HB) as h:
                        V.tensor_scalar(idxT["key"][:, :, 0:NG], idxT["hi"][:, :, 0:NG], 0.0, None, ALU.is_equal).then_inc(gen_step, 1)
                        with dve.Fori(0, NG) as g:
                            dve.wait_ge(gen_step, b * (2 * HB + 2) + h * 2 + NT + 1)
                            dve.wait_ge(gen_mm, NT * NG + (b * HB + h) * NG + g + 1)
                            for j in range(SUB):
                                V.tensor_scalar(oneS[0][:, j, :], iotaB[:], idxT["lo"][:, j, bass.ds(g, 1)], None, ALU.is_equal)
                                last = V.tensor_scalar(oneS[1][:, j, :], iotaB[:], idxT["dA"][:, j, bass.ds(g, 1)],
                                                       idxT["key"][:, j, bass.ds(g, 1)], ALU.is_equal, ALU.mult)
                            last.then_inc(gen_hot, 1)
                            dve.wait_ge(gen_mm, NT * NG + (b * HB + h) * NG + g + 2)
                            V.tensor_tensor(A16[:, bass.ds(h, 1), bass.ds(b * P, P)], ps[:, 0, 0:P].rearrange("p (a d) -> p a d", a=1),
                                            A16[:, bass.ds(h, 1), bass.ds(b * P, P)], ALU.add).then_inc(gen_add, 1)
                            dve.wait_ge(gen_add, NT * NG + (b * HB + h) * NG + g + 1)
                        V.tensor_scalar(idxT["hi"][:, :, 0:NG], idxT["hi"][:, :, 0:NG], -1.0, None, ALU.add).then_inc(gen_step, 1)
                        dve.wait_ge(gen_step, b * (2 * HB + 2) + h * 2 + NT + 2)
                    V.tensor_scalar(idxT["hi"][:, :, 0:NG], idxT["hi"][:, :, 0:NG], float(HB), None, ALU.add).then_inc(gen_step, 1)
                    V.tensor_scalar(idxT["dA"][:, :, 0:NG], idxT["dA"][:, :, 0:NG], float(-P), None, ALU.add).then_inc(gen_step, 1)
                    dve.wait_ge(gen_step, (b + 1) * (2 * HB + 2) + NT)
                V.nop()
            V.nop().then_inc(summed, 1)

            dve.wait_ge(summed, 1)

            def u1(b):
                dve.wait_ge(u1_mm, b + 1)
                V.tensor_tensor(U[:, b, :], ps[:, b % 3, :], buB[:], ALU.add).then_inc(u1_done, 1)

            f = fold
            V.tensor_tensor(f[:], A16[:, 0:5, 0:NP], A16[:, 5:10, 0:NP], ALU.add).then_inc(fold_step, 1)
            u1(0)
            dve.wait_ge(fold_step, 1)
            V.tensor_tensor(f[:, 0:2, :], f[:, 0:2, :], f[:, 2:4, :], ALU.add).then_inc(fold_step, 1)
            dve.wait_ge(fold_step, 2)
            V.tensor_tensor(f[:, 0, :], f[:, 0, :], f[:, 1, :], ALU.add).then_inc(fold_step, 1)
            u1(1)
            dve.wait_ge(fold_step, 3)
            V.tensor_tensor(Dsum[:], f[:, 0, :], f[:, 4, :], ALU.add).then_inc(dsum_ready, 1)
            dve.wait_ge(dsum_ready, 1)
            V.tensor_reduce(most[:], Dsum[:], AX.X, ALU.max).then_inc(fold_step, 1)
            for b in range(2, 5):
                u1(b)
            dve.wait_ge(most_mm, 1)
            V.tensor_reduce(most1_f[0:1, 0:1], ps[0:1, 4, 0:P], AX.X, ALU.max).then_inc(most_ready, 1)
            dve.wait_ge(most_ready, 1)
            V.tensor_copy(most1[0:1, 0:1], most1_f[0:1, 0:1]).then_inc(most_ready, 1)
            dve.wait_ge(deg_mm, 1)
            V.tensor_scalar(degs[:], ps[:, 5, 0:NT], 1.0, None, ALU.max).then_inc(deg_step, 1)
            V.tensor_scalar(has[:], ps[:, 5, 0:NT], 1.0, None, ALU.min).then_inc(deg_step, 1)
            dve.wait_ge(deg_step, 2)
            V.reciprocal(rdeg[:], degs[:]).then_inc(deg_step, 1)
            for b in range(5, NT):
                u1(b)
            for b in range(NW1, NT):
                dve.wait_ge(hi0_ready, b + 1)
                ins = V.tensor_tensor(Hl[:, b, :], X[:, b, :], Hh[:, b, :].bitcast(F32), ALU.subtract)
            ins.then_inc(low0_ready[1], 1)
            dve.wait_ge(u1_done, NT)
            dve.wait_ge(ct_done, FC + 1)
            for b in range(NT):
                V.scalar_tensor_tensor(U[:, b, :], cbB[:], has[:, b:b + 1], U[:, b, :], ALU.mult, ALU.add).then_inc(deg_step, 1)
            dve.wait_ge(deg_step, 3 + NT)
            for n in range((NW + 1) // 2, NW):
                w = WINDOWS[n]
                part = aggT[:, :, w * HALF:w * HALF + P]
                dve.wait_ge(win_mm, n + 1)
                dve.wait_ge(win_done, (NW + 1) // 2)
                V.tensor_tensor(part, ps[:, 6 + n % 2, :].rearrange("p (f n) -> p f n", f=FC), part, ALU.add).then_inc(win_done, 1)
            dve.wait_ge(win_done, NW)

            def packed(first):
                return ps[:, first:first + 2, :].rearrange("p k (g n) -> p (k g) n", g=2)

            def add_sums(products, start):
                part = aggT[:, :, start:start + products.shape[-1]]
                return V.tensor_tensor(part, products, part, ALU.add)

            dve.wait_ge(agg_mm, 1)
            add_sums(ps[:, 0:FC, :], 0).then_inc(agg_done, 1)
            dve.wait_ge(agg_mm, 2)
            add_sums(packed(6), QS[2][0]).then_inc(agg_done, 1)

            def update(b):
                dve.wait_ge(c_mm, b + 1)
                V.scalar_tensor_tensor(tt[b % TB][:], ps[:, 4 + b % 2, :], rdeg[:, ORDER[b]:ORDER[b] + 1], U[:, ORDER[b], :], ALU.mult, ALU.add).then_inc(t_ready, 1)

            def add_h0(b):
                dve.wait_ge(g_ready, b + 1)
                dve.wait_ge(h0t_ready, b + 1)
                V.tensor_tensor(tt[b % TB][:], tt[b % TB][:], h0t[b % TB][:], ALU.add).then_inc(o_sum, 1)

            def o_moments(b):
                dve.wait_ge(o_sum, b + 1)
                V.bn_stats(stats[:, b, :], tt[b % TB][:]).then_inc(o_stats, 1)

            def o_moments2(b):
                dve.wait_ge(o_stats, b + 1)
                V.bn_aggr(mv[:, b, :], stats[:, b, :]).then_inc(o_aggr, 1)

            def o_variance(b):
                dve.wait_ge(o_aggr, b + 1)
                V.tensor_scalar(ve[:, b:b + 1], mv[:, b, 1:2], EPS, None, ALU.add).then_inc(ve1_ready, 1)

            def center(b):
                dve.wait_ge(o_aggr, b + 1)
                V.scalar_tensor_tensor(tt[b % TB][:], tt[b % TB][:], mv[:, b, 0:1], gammaB[:], ALU.subtract, ALU.mult).then_inc(centered, 1)

            def add_x(b):
                dve.wait_ge(centered, b + 1)
                dve.wait_ge(rs1_ready, b + 1)
                dve.wait_ge(xb_ready, b + 1)
                V.scalar_tensor_tensor(U[:, ORDER[b], :], tt[b % TB][:], rs[:, b:b + 1], xt[b % TB][:], ALU.mult, ALU.add).then_inc(x1_ready, 1)

            def x1_moments(b):
                dve.wait_ge(x1_ready, b + 1)
                V.bn_stats(stats2[:, b, :], U[:, ORDER[b], :]).then_inc(x1_stats, 1)

            def x1_moments2(b):
                dve.wait_ge(x1_stats, b + 1)
                V.bn_aggr(mv2[:, b, :], stats2[:, b, :]).then_inc(x1_aggr, 1)

            def x1_variance(b):
                dve.wait_ge(x1_aggr, b + 1)
                V.tensor_scalar(ve2[:, b:b + 1], mv2[:, b, 1:2], EPS, None, ALU.add).then_inc(ve2_ready, 1)

            def shift(b):
                dve.wait_ge(rs2_ready, b + 1)
                V.scalar_tensor_tensor(nb[:, b:b + 1], mv2[:, b, 0:1], -1.0, rs2[:, b:b + 1], ALU.mult, ALU.mult).then_inc(nb2_ready, 1)

            def low_h1(b):
                dve.wait_ge(hi1_ready, b + 1)
                dve.wait_ge(h1T_mm, b + 1)
                V.tensor_tensor(Hl[:, ORDER[b], :], X[:, ORDER[b], :], Hh[:, ORDER[b], :].bitcast(F32), ALU.subtract).then_inc(split1, 1)

            dve.wait_ge(late_in, 48)
            STEPS = [(update, 0), (center, 2), (add_h0, 1), (add_x, 2), (o_moments, 1), (shift, 3), (x1_moments, 2), (o_moments2, 1),
                     (x1_moments2, 2), (o_variance, 1), (x1_variance, 2), (low_h1, 4)]
            for k in range(SLOT[-1] + 5):
                if k == SLOT[EARLY] - 1:
                    dve.wait_ge(ab_mm, NT)
                    for first, end in ((0, P), (P, 512)):
                        add_sums(ps[:, 0:FC, first:end], QS[1][0] + first).then_inc(agg_done, 1)
                for work, lag in STEPS:
                    if k - lag in SLOT:
                        work(SLOT.index(k - lag))

            dve.wait_ge(h1T_done, NT)
            for n, (products, start) in enumerate(((ps[:, 0:FC, :], 0), (packed(4), QS[1][0]), (packed(6), QS[1][0] + 256), (packed(4), QS[2][0]))):
                dve.wait_ge(rst_mm, n + 1)
                add_sums(products, start).then_inc(rst_done, 1)
            for b in range(NT):
                dve.wait_ge(y_mm, b + 1)
                dve.wait_ge(res_step, 3 * b + 3)
                rows = P if b < NT - 1 else TAIL
                V.tensor_tensor(U[0:rows, b, :], ps[0:rows, 4 + b % 2, :], U[0:rows, b, :], ALU.add).then_inc(y_done, 1)

        @block.tensor
        def _(pe):
            T = nc.tensor
            pe.wait_ge(ident_ready, 1)
            pe.wait_ge(wu2_in, 16)

            def transpose_wu(n):
                k = WU_ORDER[n]
                for o in range(FC):
                    last = T.transpose(ps[:, 6 + n % 2, o * P:(o + 1) * P], WuN[:, o, k * P:(k + 1) * P], ident[:])
                last.then_inc(wuT_mm, 1)

            for n in range(2 * FC):
                if n == FC:
                    pe.wait_ge(wu1_in, 16)
                if n >= 2:
                    pe.wait_ge(wuT_done, n - 1)
                transpose_wu(n)
            pe.wait_ge(wuT_done, 2 * FC)
            T.sem_inc(group_done, SLOTS)
            pe.wait_ge(wm_in, 16)

            def product(k):
                for m in range(FC):
                    last = T.matmul(ps[:, 6 + k % 2, :], WmN[:, m, k * P:(k + 1) * P] if k < FC else bmB[:, m, :], Wu2T[:, m, :],
                                    start=m == 0, stop=m == FC - 1)
                last.then_inc(ct_mm, 1)

            def transpose_indices(quantities, q):
                for name, mine in quantities:
                    if name == "dE":
                        pe.wait_ge(outside_ready, 5)
                    for j in range(SUB):
                        cols = slice(j, GE, SUB) if name in ("drel", "dE") else slice(j * P, (j + 1) * P)
                        last = T.transpose(ps[:, q, j * GP:j * GP + NG], mine[0:NG, cols], ident[0:NG, 0:NG])
                    last.then_inc(idxT_mm, 1)
                    q += 1

            product(0)
            product(1)
            pe.wait_ge(prep, PREP_KEYS)
            transpose_indices((("drel", drel), ("key", key), ("lo", lo_f)), 0)
            pe.wait_ge(ct_done, 1)
            product(2)
            transpose_indices((("hi", hi_f), ("dE", dE), ("dA", dA)), 3)
            pe.wait_ge(ct_done, 2)
            product(3)
            pe.wait_ge(ct_done, 3)
            pe.wait_ge(idxT_out, 3)
            pe.wait_ge(idxT_done, 3)

            def group(s, n, turn):
                h = s % HOTS
                pe.wait_ge(add_step, (n + 1) * SUB)
                pe.wait_ge(sum_step, n + 1)
                pe.wait_ge(hotD_ready, 2 * n + 2)
                pe.wait_ge(ea_in[s], 16 * (turn + 1))
                for j in range(2):
                    T.matmul(ps[:, s, :], oneD[h][:, j, :].bitcast(F32), ea[s][:, j, :], start=j == 0, stop=False)
                pe.wait_ge(hotK_ready, n + 1)
                pe.wait_ge(hotA_ready, n + 1)
                for j in range(SUB):
                    T.matmul(ps[:, 4 + s, j * KW:(j + 1) * KW], oneS[h][:, j, :], oneK[h][:, j, :], start=True, stop=True)
                pe.wait_ge(hi_ready, n + 1)
                for j in range(2):
                    T.matmul(ps[:, s, :], oneD[h][:, 2 + j, :], hi[h][:, j, :], start=False, stop=False)
                pe.wait_ge(lo_ready, n + 1)
                for j in range(2):
                    last = T.matmul(ps[:, s, :], oneD[h][:, 2 + j, :], lo[h][:, j, :], start=False, stop=j == 1)
                last.then_inc(group_done, 1)

            pe.wait_ge(bmB_done, 1)
            for first, end in ((0, SPLIT), (SPLIT, TURNS)):
                with pe.Fori(first, end) as i:
                    for r in range(ROUND):
                        group(r % SLOTS, i * ROUND + r, i * (ROUND // SLOTS) + r // SLOTS)
                if first == 0:
                    pe.wait_ge(add_step, (SPLIT * ROUND - 1 + SLOTS) * SUB)
                    product(FC)
            for n in range(PEELED, NG):
                group(n % SLOTS, n, n // SLOTS)

            def transpose_h0(b):
                pe.wait_ge(h0_ready, b + 1)
                if b >= 2:
                    pe.wait_ge(hT_done, b - 1)
                for f in range(FC):
                    last = T.transpose(ps[:, 3 + 4 * (b % 2), f * P:(f + 1) * P], X[:, b, f * P:(f + 1) * P], ident[:])
                last.then_inc(hT_mm, 1)

            assert (NG - SLOTS) % SLOTS == 3
            pe.wait_ge(add_step, NG * SUB)
            pe.wait_ge(sum_step, NG)
            transpose_h0(0)
            transpose_h0(1)

            pe.wait_ge(prep, PREP_ALL)
            uncovered = pe.value_load(nunc[0:1, 0:1], min_val=0, max_val=2 * E)
            with pe.If(uncovered > 0):
                pe.wait_ge(add_step, (NG + SLOTS) * SUB)
                pe.wait_ge(sum_step, NG + SLOTS)
                T.sem_inc(gen_mm, 1)
                with pe.Fori(0, NT * NG) as n:
                    pe.wait_ge(gen_ea_in, 16 * n + 16)
                    pe.wait_ge(gen_hot, n + 1)
                    for j in range(SUB):
                        last = T.matmul(ps[:, 0, :], oneD[0][:, j, :].bitcast(F32), ea[0][:, j, :], start=j == 0, stop=j == SUB - 1)
                    last.then_inc(gen_mm, 1)
                with pe.Fori(0, NT * HB * NG) as n:
                    pe.wait_ge(gen_hot, n + NT * NG + 1)
                    for j in range(SUB):
                        last = T.matmul(ps[:, 0, 0:P], oneS[0][:, j, :], oneS[1][:, j, :], start=j == 0, stop=j == SUB - 1)
                    last.then_inc(gen_mm, 1)
                pe.wait_ge(gen_add, NT * NG * (1 + HB))

            for b in range(NT):
                if b == 4:
                    pe.wait_ge(fold_step, 4)
                    T.transpose(ps[0:1, 4, 0:P], most[:], ident[:]).then_inc(most_mm, 1)
                    for d in range(NT):
                        last = T.matmul(ps[:, 5, d:d + 1], Dsum[:, d * P:(d + 1) * P], onesF[:, 0:1], start=True, stop=True)
                    last.then_inc(deg_mm, 1)
                if b == NT - 1:
                    pe.wait_ge(most_ready, 2)
                    large = pe.value_load(most1[0:1, 0:1], min_val=0, max_val=E + P)
                if b >= 3:
                    pe.wait_ge(u1_done, b - 2)
                if b < 3:
                    pe.wait_ge(add_step, (NG - 2 + b + SLOTS) * SUB)
                    pe.wait_ge(sum_step, NG - 2 + b + SLOTS)
                pe.wait_ge(hT_done, b + 1)
                for f in range(FC):
                    last = T.matmul(ps[:, b % 3, :], U[:, b, f * P:(f + 1) * P], Wu1T[:, f, :], start=f == 0, stop=f == FC - 1)
                last.then_inc(u1_mm, 1)
                if b + 2 < NT:
                    transpose_h0(b + 2)

            def bank(chunk, f, lo, hi):
                if chunk in ("A", "AB"):
                    return ps[:, f, lo:hi]
                first = 4 if chunk in ("B", "E") else 6
                return ps[:, first + f // 2, (f % 2) * 256 + lo:(f % 2) * 256 + hi]

            NODES = {"A": QS[0], "AB": QS[1], "D": QS[2], "E": QS[2], "B": (QS[1][0], 256), "C": (QS[1][0] + 256, 256)}

            def times_A(exact, c, chunk, first_c, last_c):
                start, cols = NODES[chunk]
                for f in range(FC):
                    to, rows = bank(chunk, f, 0, cols), slice(f * P, (f + 1) * P)
                    start_bank = first_c and (cols == 512 or f % 2 == 0)
                    stop_bank = last_c and (cols == 512 or f % 2 == 1)
                    if exact:
                        T.matmul(to, Hh[:, c, rows].bitcast(F32), AF[:, c, start:start + cols], start=start_bank, stop=False)
                        last = T.matmul(to, Hl[:, c, rows].bitcast(F32), AF[:, c, start:start + cols], start=False, stop=stop_bank)
                    else:
                        T.matmul(to, Hh[:, c, rows], AR[:, c, start:start + cols], start=start_bank, stop=False)
                        last = T.matmul(to, Hl[:, c, rows], AR[:, c, start:start + cols], start=False, stop=stop_bank)
                return last

            def window(n):
                if n >= 2:
                    pe.wait_ge(win_done, n - 1)
                for f in range(FC):
                    last = T.transpose(ps[:, 6 + n % 2, f * P:(f + 1) * P], SW[:, WINDOWS[n], f * P:(f + 1) * P], ident[:])
                last.then_inc(win_mm, 1)

            def transpose_h1(b):
                t = ORDER[b]
                pe.wait_ge(h1_ready, b + 1)
                if b >= 2:
                    pe.wait_ge(h1T_done, b - 1)
                for f in range(FC):
                    last = T.transpose(ps[:, 6 + b % 2, f * P:(f + 1) * P], X[:, t, f * P:(f + 1) * P], ident[:])
                last.then_inc(h1T_mm, 1)

            def map_agg(b):
                if b >= 2:
                    pe.wait_ge(t_ready, b - 1)
                for f in range(FC):
                    last = T.matmul(ps[:, 4 + b % 2, :], aggT[:, f, ORDER[b] * P:(ORDER[b] + 1) * P], CT[:, f, :], start=f == 0, stop=f == FC - 1)
                last.then_inc(c_mm, 1)

            def layers(exact):
                if exact:
                    pe.wait_ge(conv_exact, 1)
                pe.wait_ge(conv, NT)
                pe.wait_ge(u1_done, NT)
                for c in range(NT):
                    if c < NW1:
                        pe.wait_ge(low0_ready[0], c + 1)
                    elif c == NW1:
                        pe.wait_ge(low0_ready[1], 1)
                    last = times_A(exact, c, "A", c == 0, c == NT - 1)
                    if c == NT - 1:
                        last.then_inc(agg_mm, 1)
                    for n in range(2 * c + (c > 0), min(2 * c + 3, NW)):
                        window(n)
                pe.wait_ge(win_done, NW)
                pe.wait_ge(deg_step, 2)
                for c in range(NT):
                    last = times_A(exact, c, "D", c == 0, c == NT - 1)
                last.then_inc(agg_mm, 1)

                def enter(b, chunks):
                    pe.wait_ge(split1, b + 1)
                    for chunk in chunks:
                        last = times_A(exact, ORDER[b], chunk, b == 0, b == NT - 1)
                    return last

                pe.wait_ge(agg_done, 1)
                for c in range(NT):
                    times_A(exact, ORDER[c], "AB", c == 0, c == NT - 1).then_inc(ab_mm, 1)
                    if c == 4:
                        pe.wait_ge(agg_done, 2)
                    if c < EARLY:
                        map_agg(c)
                    if c in H1_AT:
                        transpose_h1(H1_AT.index(c))
                pe.wait_ge(agg_done, 3)
                for b in range(EARLY, NT):
                    map_agg(b)
                    if b == EARLY:
                        pe.wait_ge(agg_done, 4)
                    enter(b - EARLY, "A")
                    if b - EARLY + len(H1_AT) < EARLY:
                        transpose_h1(b - EARLY + len(H1_AT))
                pe.wait_ge(t_ready, NT)
                assert NT == 10 and EARLY == 6
                for step in ("A4", "T6", "A5", "B0", "B1", "T7", "B2", "B3", "B4", "T8", "B5", "T9"):
                    if step[0] == "T":
                        transpose_h1(int(step[1]))
                    else:
                        enter(int(step[1]), step[0])
                for b in range(EARLY, NT):
                    last = enter(b, "A")
                    if b == NT - 1:
                        last.then_inc(rst_mm, 1)
                    last = enter(b, "B")
                last.then_inc(rst_mm, 1)
                pe.wait_ge(h1T_done, NT)
                for b in range(NT):
                    last = enter(b, "C")
                last.then_inc(rst_mm, 1)
                pe.wait_ge(rst_done, 2)
                for b in range(NT):
                    last = enter(b, "E")
                last.then_inc(rst_mm, 1)

            with pe.If(large > COUNT_MAX):
                layers(True)
            with pe.Else():
                layers(False)
            pe.wait_ge(w12_in, 32)
            pe.wait_ge(rst_done, 2)
            T.sem_inc(hid_done, 4)

            def hidden(start, cols, n):
                for k in range(KC):
                    pe.wait_ge(hid_done, n * KC + k + 1)
                    for f in range(FC):
                        last = T.matmul(ps[:, k % 4, 0:cols], W1s[:, f, k * P:(k + 1) * P], aggT[:, f, bass.ds(start, cols)],
                                        start=f == 0, stop=f == FC - 1)
                    last.then_inc(hid_mm, 1)

            with pe.Fori(0, NQ - 1) as q:
                pe.wait_ge(rst_done, 2 * q + 2)
                hidden(q * 512, 512, q)
            hidden(QS[-1][0], N - QS[-1][0], NQ - 1)
            for b in range(NT):
                pe.wait_ge(hid_done, (b * P // 512 + 1) * KC + 4)
                if b >= 2:
                    pe.wait_ge(y_done, b - 1)
                rows = P if b < NT - 1 else TAIL
                for k in range(KC):
                    last = T.matmul(ps[0:rows, 4 + b % 2, :], hid[:, k, b * P:b * P + rows], W2s[:, k, :], start=k == 0, stop=k == KC - 1)
                last.then_inc(y_mm, 1)


_INS = ['x', 'src', 'dst', 'edge_attr_512', 'L0_gnn_Wm', 'L0_gnn_bm', 'L0_gnn_Wu', 'L0_gnn_bu', 'L0_gnn_gamma',
        'L0_gnn_beta', 'L1_gnn_W1', 'L1_gnn_b1', 'L1_gnn_W2', 'L1_gnn_b2', 'L1_gnn_eps']
_OUTS = [((1250, 512), 'float32')]


def kernel(**inputs):
    import numpy as _np
    import concourse.bacc as _bacc
    from concourse import mybir as _mybir
    from concourse.bass_utils import run_bass_kernel_spmd as _run

    nc = _bacc.Bacc("TRN2", target_bir_lowering=False, num_devices=1)
    arrays, args = {}, []
    for name in _INS:
        a = _np.ascontiguousarray(inputs[name])
        arrays[f"in_{name}_dram"] = a
        args.append(nc.dram_tensor(f"in_{name}_dram", a.shape, _mybir.dt.from_np(a.dtype), kind="ExternalInput").ap())
    for i, (shape, dtype) in enumerate(_OUTS):
        dt = _mybir.dt.from_np(_np.dtype(dtype))
        args.append(nc.dram_tensor(f"out_{i}_dram", shape, dt, kind="ExternalOutput").ap())
    gnn_kernel(nc, *args)
    r = _run(nc, [arrays], core_ids=[0])
    return r.results[0]["out_0_dram"]
```
